# Optimizing a Trainium2 kernel written in Bass

```python
import numpy as np
import jax
import jax.numpy as jnp

def _softmax(x, axis=-1):
    return jax.nn.softmax(x, axis=axis)

def _gelu(x):
    return jax.nn.gelu(x, approximate=True)

def _silu(x):
    return jax.nn.silu(x)

def _sigmoid(x):
    return jax.nn.sigmoid(x)

def _layernorm(x, axis=-1, eps=1e-05):
    m = jnp.mean(x, axis=axis, keepdims=True)
    v = jnp.var(x, axis=axis, keepdims=True)
    return (x - m) / jnp.sqrt(v + eps)

def _scatter_add(tgt, idx, src, axis=0):
    return tgt.at[idx].add(src)

def _segment_sum(src, seg, n):
    return jax.ops.segment_sum(src, seg, n)
kernel_name = 'mk_adj_preln_d2_adj_r2_3afb1b'

def setup_inputs(seed: int=0):
    np.random.seed(seed)
    _w = jnp.asarray

    def _rec_inputs():
        import jax
        import jax.numpy as jnp
        _gk = jax.random.key(seed)
        x = 7.22e-05 + 1 * jax.random.normal(jax.random.fold_in(_gk, 1), (32, 256, 128), jnp.float32)
        _w = (1.0 + jnp.arange(256, dtype=jnp.float32)) ** (-0.5)
        _w = _w / _w.mean()
        _pij = jnp.clip(0.03125 * _w[:, None] * _w[None, :], 0.0, 1.0)
        _a = jax.random.uniform(jax.random.fold_in(_gk, 2), (32, 256, 256)) < _pij
        _a = jnp.logical_or(_a, jnp.swapaxes(_a, -1, -2))
        _a = jnp.logical_or(_a, jnp.eye(256, dtype=bool))
        _af = _a.astype(jnp.float32)
        adj = _af
        return (x, adj)
    x, adj = _rec_inputs()

    def _L0_gnn_setup():
        import jax, jax.numpy as jnp
        import numpy as np
        from jax import lax
        DIM = 128
        EPS = 1e-05

        def _bn(h, g, b, m, v):
            scale = g / jnp.sqrt(v + EPS)
            return h * scale[None, :, None] + (b - m * scale)[None, :, None]

        def _conv1d(h, w, pad):
            return lax.conv_general_dilated(h, w, window_strides=(1,), padding=[(pad, pad)], dimension_numbers=('NCH', 'OIH', 'NCH'))
        key = jax.random.key(seed)
        ks = jax.random.split(key, 16)
        bs, n, d = (16, 1024, DIM)
        s = 0.05
        return {'x': jax.random.normal(ks[0], (bs, n, d), jnp.float32), 'mask': jnp.ones((bs, n, n), jnp.float32), 'w_se': jax.random.normal(ks[1], (3, d), jnp.float32) * s, 'b_se': jnp.zeros((3,), jnp.float32), 'conv1_w': jax.random.normal(ks[2], (d, d, 1), jnp.float32) * s, 'bn1_g': jnp.ones((d,), jnp.float32), 'bn1_b': jnp.zeros((d,), jnp.float32), 'bn1_m': jnp.zeros((d,), jnp.float32), 'bn1_v': jnp.ones((d,), jnp.float32), 'conv2_w': jax.random.normal(ks[3], (d, d, 17), jnp.float32) * s, 'bn2_g': jnp.ones((d,), jnp.float32), 'bn2_b': jnp.zeros((d,), jnp.float32), 'bn2_m': jnp.zeros((d,), jnp.float32), 'bn2_v': jnp.ones((d,), jnp.float32), 'w_msg': jax.random.normal(ks[4], (d, d), jnp.float32) * s, 'b_msg': jnp.zeros((d,), jnp.float32), 'w_ih': jax.random.normal(ks[5], (3 * d, 2 * d), jnp.float32) * s, 'b_ih': jnp.zeros((3 * d,), jnp.float32), 'w_hh': jax.random.normal(ks[6], (3 * d, d), jnp.float32) * s, 'b_hh': jnp.zeros((3 * d,), jnp.float32)}
    _L0_gnn_all = _L0_gnn_setup()
    _L0_gnn_in = {k: v for k, v in _L0_gnn_all.items() if k in ('w_se', 'b_se', 'conv1_w', 'bn1_g', 'bn1_b', 'bn1_m', 'bn1_v', 'conv2_w', 'bn2_g', 'bn2_b', 'bn2_m', 'bn2_v', 'w_msg', 'b_msg', 'w_ih', 'b_ih', 'w_hh', 'b_hh')}
    del _L0_gnn_all

    def _L1_gnn_setup():
        import jax, jax.numpy as jnp
        import numpy as np
        NEG_SLOPE = -0.2
        MASK_VAL = -9000000000000000.0
        key = jax.random.key(seed)
        k1, k2, k3, k4 = jax.random.split(key, 4)
        B, N, F, O = (8, 1024, 128, 128)
        x = jax.random.normal(k1, (B, N, F), dtype=jnp.float32)
        adj = jax.random.normal(k2, (B, N, N), dtype=jnp.float32)
        bw = 1.414 * np.sqrt(6.0 / (F + O))
        W_a = jax.random.uniform(k3, (F, O), minval=-bw, maxval=bw, dtype=jnp.float32)
        bb = 1.414 * np.sqrt(6.0 / (1 + O))
        bias = jax.random.uniform(k4, (1, O), minval=-bb, maxval=bb, dtype=jnp.float32)
        return {'x': x, 'adj': adj, 'W_a': W_a, 'bias': bias}
    _L1_gnn_all = _L1_gnn_setup()
    _L1_gnn_in = {k: v for k, v in _L1_gnn_all.items() if k in ('W_a', 'bias')}
    del _L1_gnn_all
    return {'x': x, 'adj': adj, 'L0_gnn_w_se': _L0_gnn_in['w_se'], 'L0_gnn_b_se': _L0_gnn_in['b_se'], 'L0_gnn_conv1_w': _L0_gnn_in['conv1_w'], 'L0_gnn_bn1_g': _L0_gnn_in['bn1_g'], 'L0_gnn_bn1_b': _L0_gnn_in['bn1_b'], 'L0_gnn_bn1_m': _L0_gnn_in['bn1_m'], 'L0_gnn_bn1_v': _L0_gnn_in['bn1_v'], 'L0_gnn_conv2_w': _L0_gnn_in['conv2_w'], 'L0_gnn_bn2_g': _L0_gnn_in['bn2_g'], 'L0_gnn_bn2_b': _L0_gnn_in['bn2_b'], 'L0_gnn_bn2_m': _L0_gnn_in['bn2_m'], 'L0_gnn_bn2_v': _L0_gnn_in['bn2_v'], 'L0_gnn_w_msg': _L0_gnn_in['w_msg'], 'L0_gnn_b_msg': _L0_gnn_in['b_msg'], 'L0_gnn_w_ih': _L0_gnn_in['w_ih'], 'L0_gnn_b_ih': _L0_gnn_in['b_ih'], 'L0_gnn_w_hh': _L0_gnn_in['w_hh'], 'L0_gnn_b_hh': _L0_gnn_in['b_hh'], 'L1_gnn_W_a': _L1_gnn_in['W_a'], 'L1_gnn_bias': _L1_gnn_in['bias']}

def reference(x, adj, L0_gnn_w_se, L0_gnn_b_se, L0_gnn_conv1_w, L0_gnn_bn1_g, L0_gnn_bn1_b, L0_gnn_bn1_m, L0_gnn_bn1_v, L0_gnn_conv2_w, L0_gnn_bn2_g, L0_gnn_bn2_b, L0_gnn_bn2_m, L0_gnn_bn2_v, L0_gnn_w_msg, L0_gnn_b_msg, L0_gnn_w_ih, L0_gnn_b_ih, L0_gnn_w_hh, L0_gnn_b_hh, L1_gnn_W_a, L1_gnn_bias):
    import jax
    import jax.numpy as jnp

    def _L0_gnn_ref(x, mask, w_se, b_se, conv1_w, bn1_g, bn1_b, bn1_m, bn1_v, conv2_w, bn2_g, bn2_b, bn2_m, bn2_v, w_msg, b_msg, w_ih, b_ih, w_hh, b_hh):
        import jax, jax.numpy as jnp
        import numpy as np
        from jax import lax
        DIM = 128
        EPS = 1e-05

        def _bn(h, g, b, m, v):
            scale = g / jnp.sqrt(v + EPS)
            return h * scale[None, :, None] + (b - m * scale)[None, :, None]

        def _conv1d(h, w, pad):
            return lax.conv_general_dilated(h, w, window_strides=(1,), padding=[(pad, pad)], dimension_numbers=('NCH', 'OIH', 'NCH'))
        d = x.shape[-1]
        xc = jnp.transpose(x, (0, 2, 1))
        h = _bn(_conv1d(xc, conv1_w, 0), bn1_g, bn1_b, bn1_m, bn1_v)
        h = jax.nn.relu(h)
        h = _bn(_conv1d(h, conv2_w, 8), bn2_g, bn2_b, bn2_m, bn2_v)
        x_conv = jnp.transpose(jax.nn.relu(h + xc), (0, 2, 1))
        s = x @ w_se.T + b_se
        sq = jnp.sum(s * s, axis=-1)
        dist = sq[:, :, None] + sq[:, None, :] - 2.0 * jnp.einsum('bnd,bmd->bnm', s, s)
        A = jnp.exp(-dist) * mask
        msg = jax.nn.relu(x @ w_msg.T + b_msg)
        x_nmp = jnp.einsum('bnm,bmd->bnd', A, msg)
        x_in = jnp.concatenate([x_conv, x_nmp], axis=-1)
        gi = x_in @ w_ih.T + b_ih
        gh = x @ w_hh.T + b_hh
        gi_r, gi_z, gi_n = (gi[..., :d], gi[..., d:2 * d], gi[..., 2 * d:])
        gh_r, gh_z, gh_n = (gh[..., :d], gh[..., d:2 * d], gh[..., 2 * d:])
        r = jax.nn.sigmoid(gi_r + gh_r)
        z = jax.nn.sigmoid(gi_z + gh_z)
        nn_ = jnp.tanh(gi_n + r * gh_n)
        return (1.0 - z) * nn_ + z * x

    def _L1_gnn_ref(x, adj, W_a, bias):
        import jax, jax.numpy as jnp
        import numpy as np
        NEG_SLOPE = -0.2
        MASK_VAL = -9000000000000000.0
        Xp = jnp.einsum('bnf,fo->bno', x, W_a)
        A = jnp.einsum('bno,bmo->bnm', Xp, Xp)
        mag = jnp.linalg.norm(A, axis=2, keepdims=True)
        A = A / (mag * jnp.swapaxes(mag, 1, 2))
        e = jnp.where(A >= 0, A, NEG_SLOPE * A)
        att = jnp.where(adj > 0, e, MASK_VAL)
        att = jax.nn.softmax(att, axis=2)
        h = jnp.einsum('bnm,bmf->bnf', att, x) + bias
        return jax.nn.elu(h)
    h = jnp.maximum(_layernorm(x, axis=-1), 0.0)
    x = x + _L0_gnn_ref(h, adj, L0_gnn_w_se, L0_gnn_b_se, L0_gnn_conv1_w, L0_gnn_bn1_g, L0_gnn_bn1_b, L0_gnn_bn1_m, L0_gnn_bn1_v, L0_gnn_conv2_w, L0_gnn_bn2_g, L0_gnn_bn2_b, L0_gnn_bn2_m, L0_gnn_bn2_v, L0_gnn_w_msg, L0_gnn_b_msg, L0_gnn_w_ih, L0_gnn_b_ih, L0_gnn_w_hh, L0_gnn_b_hh)
    h = jnp.maximum(_layernorm(x, axis=-1), 0.0)
    x = x + _L1_gnn_ref(h, adj, L1_gnn_W_a, L1_gnn_bias)
    return x

_drawn_inputs = setup_inputs


def setup_inputs(seed=0):
    import zlib

    import numpy as np

    out = dict(_drawn_inputs(seed))
    spreads = {'L0_gnn_b_se': (0.0, 2.0),
     'L0_gnn_bn1_g': (1.0, 0.6),
     'L0_gnn_bn1_b': (0.0, 0.402),
     'L0_gnn_bn1_m': (0.0, 0.391),
     'L0_gnn_bn1_v': (1.0, 0.6),
     'L0_gnn_bn2_g': (1.0, 0.6),
     'L0_gnn_bn2_b': (0.0, 0.609),
     'L0_gnn_bn2_m': (0.0, 0.555),
     'L0_gnn_bn2_v': (1.0, 0.6),
     'L0_gnn_b_msg': (0.0, 0.1),
     'L0_gnn_b_ih': (0.0, 0.1),
     'L0_gnn_b_hh': (0.0, 0.326)}
    factors = {'L1_gnn_W_a': 200.0}
    for name, (base, spread) in spreads.items():
        noise = np.random.default_rng([zlib.crc32(name.encode()), seed]).standard_normal(out[name].shape)
        drawn = base * np.exp(spread * noise) if base else spread * noise
        out[name] = jnp.asarray(drawn.astype(out[name].dtype))
    for name, factor in factors.items():
        out[name] = (out[name] * factor).astype(out[name].dtype)
    return out
```

```python
import concourse.bass as bass
from concourse import mybir
from contextlib import ExitStack

B, N, D = 32, 256, 128
P = 128
G = 2
PAIRS = B // G
NT = N // P
T = G * NT
C = G * N
TAPS = 17
PAD = TAPS // 2
S = 3
SQ, ONE = 32, 64
SR = ONE + S
LN_EPS = 1e-5
BN_EPS = 1e-5
SLOPE = -0.2
MASKED = -3.0e38

(BN1_G, BN1_B, BN1_M, BN1_V, BN2_G, BN2_B, BN2_M, BN2_V,
 BI_R, BI_Z, BI_N, BH_R, BH_Z, BH_N) = range(14)
NVEC = 14


def build(nc, x, adj, vec, w_se, b_se, w_c1, w_c2, w_msg, b_msg, w_ih, w_hh, w_a, bias, out):
    fp32 = mybir.dt.float32
    f32r = mybir.dt.float32r
    ALU = mybir.AluOpType
    ACT = mybir.ActivationFunctionType

    x_v = x.rearrange("(a g) (t p) d -> a p (g t) d", g=G, p=P)
    adj_v = adj.rearrange("(a g) (t p) m -> a p (g t) m", g=G, p=P)
    out_v = out.rearrange("(a g) (t p) d -> a p (g t) d", g=G, p=P)

    ctx = ExitStack()
    with ctx:
        def sb(name, shape, dt=fp32):
            return ctx.enter_context(nc.sbuf_tensor(name, shape, dt))

        def two(name, shape, dt=fp32):
            return [sb(f"{name}{s}", shape, dt) for s in range(2)]

        def sem(name):
            return ctx.enter_context(nc.semaphore(name))

        ident = sb("ident", [P, P])
        vecs = sb("vecs", [P, NVEC])
        c1_w, c1_wh, c1_wl = sb("c1_w", [P, D]), sb("c1_wh", [P, D], f32r), sb("c1_wl", [P, D], f32r)
        c2_w, c2_wh, c2_wl = (sb(n, [P, TAPS, D], dt) for n, dt in
                              (("c2_w", fp32), ("c2_wh", f32r), ("c2_wl", f32r)))
        msg_w, msg_wh, msg_wl = sb("msg_w", [P, D]), sb("msg_wh", [P, D], f32r), sb("msg_wl", [P, D], f32r)
        se_w3 = sb("se_w3", [P, S])
        se_w, se_wh, se_wl = sb("se_w", [P, SR]), sb("se_wh", [P, SR], f32r), sb("se_wl", [P, SR], f32r)
        g_w, g_wh, g_wl = (sb(n, [P, 3, 3 * D], dt) for n, dt in
                           (("g_w", fp32), ("g_wh", f32r), ("g_wl", f32r)))
        a_w = sb("a_w", [P, D])
        msg_b = sb("msg_b", [P, D])
        att_b = sb("att_b", [P, D])
        half = sb("half", [P, T])
        bn_s = sb("bn_s", [P, 2])
        bn_b = sb("bn_b", [P, 2])
        bn_t = sb("bn_t", [P, 2])
        gate_b = sb("gate_b", [P, 2])
        gate_t = sb("gate_t", [P, 2])
        se_b = sb("se_b", [SR, 1])
        l_scale, l_bias = sb("l_scale", [SR, 1]), sb("l_bias", [SR, 1])
        r_scale, r_bias = sb("r_scale", [SR, 1]), sb("r_bias", [SR, 1])

        eps = sb("eps", [P, T])
        tick_v, tick_p = sb("tick_v", [P, 1]), sb("tick_p", [P, 1])

        x_in = two("x_in", [P, T, D])
        adj_in = two("adj_in", [P, T, N])
        stat1, mv1 = sb("stat1", [P, T, 6]), sb("mv1", [P, T, 2])
        var1, rstd1 = sb("var1", [P, T]), sb("rstd1", [P, T])
        xn1 = sb("xn1", [P, T, D])
        hT = two("hT", [P, C])
        h_hi, h_lo = two("h_hi", [P, C], f32r), two("h_lo", [P, C], f32r)
        hb = two("hb", [P, C])
        c1 = sb("c1", [P, G, N])
        c1_hi = two("c1_hi", [P, G, N + 2 * PAD], f32r)
        c1_lo = two("c1_lo", [P, G, N + 2 * PAD], f32r)
        dl, dr = sb("dl", [SR, C]), sb("dr", [SR, C])
        msg0, msg = sb("msg0", [P, T, D]), sb("msg", [P, T, D])
        ed = sb("ed", [P, T, N])
        a0T = sb("a0T", [P, T, N])
        n_hi, n_lo = two("n_hi", [P, C], f32r), two("n_lo", [P, C], f32r)
        neg = two("neg", [P, T, N])
        c2 = sb("c2", [P, C])
        c_hi, c_lo = sb("c_hi", [P, C], f32r), sb("c_lo", [P, C], f32r)
        r_t, z_t, r_g, z_g = sb("r_t", [P, C]), sb("z_t", [P, C]), sb("r_g", [P, C]), sb("z_g", [P, C])
        gq, gw, nn = sb("gq", [P, C]), sb("gw", [P, C]), sb("nn", [P, C])
        dd, zd, gru = sb("dd", [P, C]), sb("zd", [P, C]), sb("gru", [P, C])
        x_res = two("x_res", [P, T, D])
        x1 = two("x1", [P, T, D])
        stat2, mv2 = sb("stat2", [P, T, 6]), sb("mv2", [P, T, 2])
        var2, rstd2 = sb("var2", [P, T]), sb("rstd2", [P, T])
        h2n, h2 = sb("h2n", [P, T, D]), sb("h2", [P, T, D])
        h2T, xpT = sb("h2T", [P, C]), sb("xpT", [P, C])
        squares = sb("squares", [P, T, N])
        mag2, imag = sb("mag2", [P, T]), sb("imag", [P, T])
        imag_row = sb("imag_row", [P, C])
        an, score, att, prob = (sb(n, [P, T, N]) for n in ("an", "score", "att", "prob"))
        rmax, nmax = sb("rmax", [P, T]), sb("nmax", [P, T])
        rsum, rinv = sb("rsum", [P, T]), sb("rinv", [P, T])
        probT = sb("probT", [P, T, N])
        u_att, u_min, u_exp, u_elu = (sb(n, [P, T, D]) for n in ("u_att", "u_min", "u_exp", "u_elu"))
        y_out = two("y_out", [P, T, D])

        bank = ctx.enter_context(nc.psum_tensor("bank", [P, 8, 512], fp32))

        def tiles(b):
            return bank[:, b, :].rearrange("p (t d) -> p t d", t=T)

        def rows(b, n=1):
            return bank[:, b:b + n, :].rearrange("p a (t m) -> p (a t) m", t=NT)

        ps_conv2 = bank[:, 0, :]
        ps_adjT = rows(1, 2)
        ps_r, ps_z, ps_hn, ps_in = (bank[:, b, :] for b in (1, 2, 3, 4))
        ps_imag = bank[:, 2, :]
        ps_dist = rows(3, 2)
        ps_conv1, ps_xp, ps_nmp = bank[:, 5, :], bank[:, 5, :], bank[:, 5, :]
        ps_pv = tiles(5)
        ps_hT, ps_h2T, ps_se = bank[:, 6, :], bank[:, 6, :], bank[0:SR, 6, :]
        ps_gruT, ps_msg = tiles(7), tiles(7)
        ps_a, ps_probT = rows(6, 2), rows(6, 2)

        x_loaded = [sem("x_loaded0"), sem("x_loaded1")]
        adj_loaded = [sem("adj_loaded0"), sem("adj_loaded1")]
        res_loaded = [sem("res_loaded0"), sem("res_loaded1")]
        stored = [sem("stored0"), sem("stored1")]
        w_vec, w_front, w_conv2, w_gate, w_back, w_seb = (
            sem(n) for n in ("w_vec", "w_front", "w_conv2", "w_gate", "w_back", "w_seb"))
        ident_made, se_cleared, se_spread, front_hi, front_lo = (
            sem(n) for n in ("ident_made", "se_cleared", "se_spread", "front_hi", "front_lo"))
        conv2_hi, conv2_lo, gate_hi, gate_lo, pads_made = (
            sem(n) for n in ("conv2_hi", "conv2_lo", "gate_hi", "gate_lo", "pads_made"))
        setup, consts_made, scales_made, dist_consts = (
            sem(n) for n in ("setup", "consts_made", "scales_made", "dist_consts"))
        stat1_done, mv1_done, var1_done, rstd1_done, xn1_done = (
            sem(n) for n in ("stat1_done", "mv1_done", "var1_done", "rstd1_done", "xn1_done"))
        hT_mm, hT_done, h_hi_done, h_lo_done, hb_done = (
            sem(n) for n in ("hT_mm", "hT_done", "h_hi_done", "h_lo_done", "hb_done"))
        conv1_mm, c1_done, c1_hi_done, c1_lo_done = (
            sem(n) for n in ("conv1_mm", "c1_done", "c1_hi_done", "c1_lo_done"))
        se_mm, dist_in, dist_sq = sem("se_mm"), sem("dist_in"), sem("dist_sq")
        msg_mm, msg0_done, msg_done = sem("msg_mm"), sem("msg0_done"), sem("msg_done")
        adjT_mm, dist_mm, ed_done, a0T_done = (sem(n) for n in ("adjT_mm", "dist_mm", "ed_done", "a0T_done"))
        nmp_mm, n_hi_done, n_lo_done, neg_done = (sem(n) for n in ("nmp_mm", "n_hi_done", "n_lo_done", "neg_done"))
        conv2_mm, c2_done, c_hi_done, c_lo_done = (sem(n) for n in ("conv2_mm", "c2_done", "c_hi_done", "c_lo_done"))
        r_mm, z_mm, in_mm = sem("r_mm"), sem("z_mm"), sem("in_mm")
        r_t_done, z_t_done, r_g_done, z_g_done = (sem(n) for n in ("r_t_done", "z_t_done", "r_g_done", "z_g_done"))
        gq_done, gw_done, nn_done, dd_done, zd_done, gru_done = (
            sem(n) for n in ("gq_done", "gw_done", "nn_done", "dd_done", "zd_done", "gru_done"))
        gruT_mm, x1_done, stat2_done, mv2_done, var2_done, rstd2_done = (
            sem(n) for n in ("gruT_mm", "x1_done", "stat2_done", "mv2_done", "var2_done", "rstd2_done"))
        h2n_done, h2_done, h2T_mm, h2T_done, xp_mm, xp_done = (
            sem(n) for n in ("h2n_done", "h2_done", "h2T_mm", "h2T_done", "xp_mm", "xp_done"))
        a_mm, mag2_done, imag_done, imag_mm, imag_row_done = (
            sem(n) for n in ("a_mm", "mag2_done", "imag_done", "imag_mm", "imag_row_done"))
        an_done, score_done, att_done, nmax_done, prob_done, rinv_done = (
            sem(n) for n in ("an_done", "score_done", "att_done", "nmax_done", "prob_done", "rinv_done"))
        probT_mm, probT_done, pv_mm = sem("probT_mm"), sem("probT_done"), sem("pv_mm")
        u_done, u_min_done, u_exp_done, u_elu_done, y_done = (
            sem(n) for n in ("u_done", "u_min_done", "u_exp_done", "u_elu_done", "y_done"))

        def done(eng, s, k):
            if not isinstance(k, int) or 0 <= k < PAIRS:
                eng.wait_ge(s, k + 1)

        def moved(eng, s, k, slot):
            if not isinstance(k, int) or 0 <= k < PAIRS:
                eng.wait_ge(s[slot], 8 * k + (8 if slot else 16))

        def steps(eng, step):
            for i in range(-2, 2):
                step(i, i % 2)
            with eng.Fori(1, PAIRS // 2 - 1) as j:
                step(2 * j, 0)
                step(2 * j + 1, 1)
            for i in range(PAIRS - 2, PAIRS + 2):
                step(i, i % 2)

        def at(i, first):
            return isinstance(i, int) and i == first

        def has(k):
            return not isinstance(k, int) or 0 <= k < PAIRS

        block = ctx.enter_context(nc.Block())

        @block.sync
        def _(sp):
            def step(i, slot):
                if has(i + 2):
                    done(sp, xn1_done, i)
                    sp.dma_start(x_in[slot][:, :, :], x_v[i + 2, :, :, :]).then_inc(x_loaded[slot], 16)
                    done(sp, neg_done, i)
                    done(sp, adjT_mm, i)
                    sp.dma_start(adj_in[slot][:, :, :], adj_v[i + 2, :, :, :]).then_inc(adj_loaded[slot], 16)
                if has(i):
                    done(sp, x1_done, i - 2)
                    sp.dma_start(x_res[slot][:, :, :], x_v[i, :, :, :]).then_inc(res_loaded[slot], 16)
                if has(i - 2):
                    done(sp, y_done, i - 2)
                    sp.dma_start(out_v[i - 2, :, :, :], y_out[slot][:, :, :]).then_inc(stored[slot], 16)

            steps(sp, step)
            for slot in range(2):
                sp.wait_ge(stored[slot], 16 * (PAIRS // 2))

        @block.gpsimd
        def _(pool):
            pool.memset(ident[:, :], 0.0).then_inc(setup, 1)
            pool.wait_ge(setup, 1)
            pool.affine_select(out=ident[:, :], in_=ident[:, :], compare_op=ALU.not_equal, fill=1.0,
                               base=0, pattern=[[-1, P]], channel_multiplier=1).then_inc(ident_made, 1)
            pool.memset(eps[:, :], LN_EPS)
            pool.memset(half[:, :], -0.5).then_inc(setup, 1)
            pool.wait_ge(w_vec, 16)
            pool.wait_ge(setup, 2)
            pool.tensor_scalar(bn_t[:, :], vecs[:, BN1_V:BN2_V + 1:BN2_V - BN1_V], 1.0, BN_EPS,
                               ALU.mult, ALU.add).then_inc(setup, 1)
            pool.wait_ge(setup, 3)
            pool.tensor_tensor(bn_s[:, :], bn_t[:, :], half[:, 0:2], ALU.pow).then_inc(setup, 1)
            pool.wait_ge(setup, 4)
            pool.tensor_tensor(bn_t[:, :], bn_s[:, :], vecs[:, BN1_G:BN2_G + 1:BN2_G - BN1_G],
                               ALU.mult).then_inc(setup, 1)
            pool.wait_ge(setup, 5)
            pool.tensor_copy(bn_s[:, :], bn_t[:, :])
            pool.tensor_tensor(bn_b[:, :], bn_t[:, :], vecs[:, BN1_M:BN2_M + 1:BN2_M - BN1_M],
                               ALU.mult).then_inc(setup, 1)
            pool.wait_ge(setup, 6)
            pool.tensor_tensor(bn_t[:, :], vecs[:, BN1_B:BN2_B + 1:BN2_B - BN1_B], bn_b[:, :],
                               ALU.subtract).then_inc(setup, 1)
            pool.wait_ge(setup, 7)
            pool.tensor_copy(bn_b[:, :], bn_t[:, :])
            pool.tensor_tensor(gate_t[:, :], vecs[:, BI_R:BI_Z + 1], vecs[:, BH_R:BH_Z + 1],
                               ALU.add).then_inc(setup, 1)
            pool.wait_ge(setup, 8)
            pool.tensor_scalar(gate_b[:, :], gate_t[:, :], 0.5, 0.0, ALU.mult, ALU.add).then_inc(consts_made, 1)
            for slot in range(2):
                for half_ in (c1_hi[slot], c1_lo[slot]):
                    pool.memset(half_[:, :, 0:PAD].bitcast(fp32), 0.0)
                    last = pool.memset(half_[:, :, PAD + N:PAD + N + PAD].bitcast(fp32), 0.0)
            last.then_inc(pads_made, 1)

            def step(i, slot):
                nxt = 1 - slot
                if at(i, 0):
                    pool.wait_ge(gate_hi, 1)
                    pool.tensor_tensor(g_wl[:, :, :], g_w[:, :, :], g_wh[:, :, :].bitcast(fp32),
                                       ALU.subtract).then_inc(gate_lo, 1)
                    pool.wait_ge(gate_lo, 1)
                if has(i + 1):
                    done(pool, z_g_done, i - 1)
                    done(pool, dist_in, i + 1)
                    pool.tensor_tensor(dl[SQ:SQ + S, :], dl[SQ:SQ + S, :], dl[SQ:SQ + S, :], ALU.mult)
                    pool.tensor_tensor(dr[ONE:ONE + S, :], dr[ONE:ONE + S, :], dr[ONE:ONE + S, :],
                                       ALU.mult).then_inc(dist_sq, 1)
                    done(pool, dist_sq, i + 1)
                if has(i - 1):
                    done(pool, mv2_done, i - 1)
                    pool.tensor_tensor(var2[:, :], mv2[:, :, 1], eps[:, :], ALU.add).then_inc(var2_done, 1)
                    done(pool, var2_done, i - 1)
                    pool.tensor_tensor(rstd2[:, :], var2[:, :], half[:, :], ALU.pow).then_inc(rstd2_done, 1)
                if has(i + 1):
                    pool.tensor_scalar(hb[nxt][:, :], hT[nxt][:, :], 1.0, bn_b[:, 1:2],
                                       ALU.mult, ALU.add).then_inc(hb_done, 1)
                    done(pool, c1_hi_done, i + 1)
                    pool.tensor_tensor(c1_lo[nxt][:, :, PAD:PAD + N], c1[:, :, :],
                                       c1_hi[nxt][:, :, PAD:PAD + N].bitcast(fp32),
                                       ALU.subtract).then_inc(c1_lo_done, 1)
                if has(i - 1):
                    done(pool, mag2_done, i - 1)
                    pool.tensor_tensor(imag[:, :], mag2[:, :], half[:, :], ALU.pow).then_inc(imag_done, 1)
                if has(i + 2):
                    done(pool, mv1_done, i + 2)
                    pool.tensor_tensor(var1[:, :], mv1[:, :, 1], eps[:, :], ALU.add).then_inc(var1_done, 1)
                    done(pool, var1_done, i + 2)
                    pool.tensor_tensor(rstd1[:, :], var1[:, :], half[:, :], ALU.pow).then_inc(rstd1_done, 1)
                if has(i):
                    done(pool, z_t_done, i)
                    pool.tensor_tensor(tick_p[:, :], half[:, 0:1], half[:, 0:1], ALU.mult)
                    pool.tensor_scalar(r_g[:, :], r_t[:, :], 0.5, 0.5, ALU.mult, ALU.add).then_inc(r_g_done, 1)
                    pool.tensor_scalar(z_g[:, :], z_t[:, :], 0.5, 0.5, ALU.mult, ALU.add).then_inc(z_g_done, 1)

            steps(pool, step)

        @block.scalar
        def _(act):
            act.dma_start(vecs[:, :], vec).then_inc(w_vec, 16)
            act.dma_start(c1_w[:, :], w_c1).then_inc(w_front, 16)
            act.dma_start(se_w3[:, :], w_se).then_inc(w_front, 16)
            act.dma_start(msg_w[:, :], w_msg).then_inc(w_front, 16)
            act.dma_start(msg_b[:, :], b_msg.broadcast_to([P, D])).then_inc(w_front, 16)
            act.dma_start(c2_w[:, :, :], w_c2).then_inc(w_conv2, 16)
            act.dma_start(g_w[:, 0:2, :], w_ih).then_inc(w_gate, 16)
            act.dma_start(g_w[:, 2, :], w_hh).then_inc(w_gate, 16)
            act.dma_start(a_w[:, :], w_a).then_inc(w_back, 16)
            act.dma_start(att_b[:, :], bias.broadcast_to([P, D])).then_inc(w_back, 16)
            act.wait_ge(se_cleared, 1)
            for row in (0, SQ, ONE):
                act.dma_start(se_b[row:row + S, :], b_se).then_inc(w_seb, 16)

            def step(i, slot):
                nxt = 1 - slot
                if at(i, -1):
                    act.wait_ge(w_conv2, 16)
                    act.activation(c2_wh[:, :, :], c2_w[:, :, :], ACT.Copy).then_inc(conv2_hi, 1)
                if at(i, 0):
                    act.wait_ge(w_gate, 32)
                    act.activation(g_wh[:, :, :], g_w[:, :, :], ACT.Copy).then_inc(gate_hi, 1)
                if has(i - 1):
                    done(act, gw_done, i - 1)
                    act.activation(nn[:, :], gw[:, :], ACT.Tanh,
                                   bias=vecs[:, BI_N:BI_N + 1]).then_inc(nn_done, 1)
                if has(i + 1):
                    done(act, hT_mm, i + 1)
                    done(act, dd_done, i - 1)
                    done(act, hb_done, i - 1)
                    done(act, h_lo_done, i - 1)
                    act.activation(hT[nxt][:, :], ps_hT, ACT.Relu).then_inc(hT_done, 1)
                if has(i - 2):
                    done(act, u_min_done, i - 2)
                    act.activation(u_exp[:, :, :], u_min[:, :, :], ACT.Exp).then_inc(u_exp_done, 1)
                if has(i + 1):
                    if at(i, -1):
                        act.wait_ge(consts_made, 1)
                        act.wait_ge(dist_consts, 2)
                    done(act, conv1_mm, i + 1)
                    done(act, c1_lo_done, i)
                    act.activation(c1[:, :, :], ps_conv1.rearrange("p (g n) -> p g n", g=G), ACT.Relu,
                                   scale=bn_s[:, 0:1], bias=bn_b[:, 0:1]).then_inc(c1_done, 1)
                    done(act, se_mm, i + 1)
                    done(act, dist_mm, i)
                    act.activation(dl[:, :], ps_se, ACT.Identity, scale=l_scale[:, :], bias=l_bias[:, :])
                    act.activation(dr[:, :], ps_se, ACT.Identity, scale=r_scale[:, :],
                                   bias=r_bias[:, :]).then_inc(dist_in, 1)
                if has(i - 1):
                    done(act, h2T_mm, i - 1)
                    act.activation(h2T[:, :], ps_h2T, ACT.Copy).then_inc(h2T_done, 1)
                    done(act, xp_mm, i - 1)
                    act.activation(xpT[:, :], ps_xp, ACT.Copy).then_inc(xp_done, 1)
                if has(i + 1):
                    done(act, dist_mm, i + 1)
                    done(act, a0T_done, i)
                    act.activation(ed[:, :, :], ps_dist, ACT.Exp).then_inc(ed_done, 1)
                if has(i - 1):
                    done(act, a_mm, i - 1)
                    done(act, imag_done, i - 2)
                    for k in range(T):
                        last = act.activation(squares[:, k, :], ps_a[:, k, :], ACT.Square,
                                              accum_out=mag2[:, k:k + 1])
                    last.then_inc(mag2_done, 1)
                if has(i + 1):
                    done(act, nmp_mm, i + 1)
                    done(act, in_mm, i - 1)
                    act.activation(n_hi[nxt][:, :], ps_nmp, ACT.Copy).then_inc(n_hi_done, 1)
                if has(i - 1):
                    done(act, imag_mm, i - 1)
                    act.activation(imag_row[:, :], ps_imag, ACT.Copy).then_inc(imag_row_done, 1)
                    done(act, nmax_done, i - 1)
                    for k in range(T):
                        last = act.activation(prob[:, k, :], att[:, k, :], ACT.Exp, bias=nmax[:, k:k + 1],
                                              accum_out=rsum[:, k:k + 1])
                    last.then_inc(prob_done, 1)
                if has(i):
                    done(act, r_mm, i)
                    done(act, r_g_done, i - 1)
                    act.activation(r_t[:, :], ps_r, ACT.Tanh, scale=0.5,
                                   bias=gate_b[:, 0:1]).then_inc(r_t_done, 1)
                    done(act, z_mm, i)
                    act.activation(z_t[:, :], ps_z, ACT.Tanh, scale=0.5,
                                   bias=gate_b[:, 1:2]).then_inc(z_t_done, 1)
                if has(i - 1):
                    done(act, probT_mm, i - 1)
                    act.activation(probT[:, :, :], ps_probT, ACT.Copy).then_inc(probT_done, 1)

            steps(act, step)

        @block.vector
        def _(dve):
            nc.vector.memset(se_w[:, :], 0.0)
            nc.vector.memset(l_scale[:, :], 1.0)
            nc.vector.memset(r_scale[:, :], 1.0)
            nc.vector.memset(se_b[:, :], 0.0).then_inc(se_cleared, 1)
            dve.wait_ge(se_cleared, 1)
            nc.vector.memset(l_scale[ONE:ONE + S, :], 0.0)
            nc.vector.memset(r_scale[0:S, :], 2.0)
            nc.vector.memset(r_scale[SQ:SQ + S, :], 0.0).then_inc(scales_made, 1)

            def carry_wait():
                nc.vector.memset(tick_v[:, :], 0.0)

            def split_weights(whole, hi, lo):
                return nc.vector.tensor_tensor(lo, whole, hi.bitcast(fp32), ALU.subtract)

            def step(i, slot):
                nxt = 1 - slot
                if at(i, -2):
                    dve.wait_ge(w_seb, 48)
                    dve.wait_ge(scales_made, 1)
                    nc.vector.tensor_copy(l_bias[:, :], se_b[:, :])
                    nc.vector.tensor_tensor(r_bias[:, :], se_b[:, :], r_scale[:, :],
                                            ALU.mult).then_inc(dist_consts, 1)
                    dve.wait_ge(dist_consts, 1)
                    nc.vector.memset(l_bias[ONE:ONE + S, :], -1.0)
                    nc.vector.memset(r_bias[SQ:SQ + S, :], -1.0).then_inc(dist_consts, 1)
                    dve.wait_ge(w_front, 64)
                    dve.wait_ge(se_cleared, 1)
                    for row in (0, SQ, ONE):
                        last = nc.vector.tensor_copy(se_w[:, row:row + S], se_w3[:, :])
                    last.then_inc(se_spread, 1)
                    dve.wait_ge(se_spread, 1)
                    nc.vector.tensor_copy(c1_wh[:, :], c1_w[:, :])
                    nc.vector.tensor_copy(msg_wh[:, :], msg_w[:, :])
                    nc.vector.tensor_copy(se_wh[:, :], se_w[:, :]).then_inc(front_hi, 1)
                    dve.wait_ge(front_hi, 1)
                    split_weights(c1_w[:, :], c1_wh[:, :], c1_wl[:, :])
                    split_weights(msg_w[:, :], msg_wh[:, :], msg_wl[:, :])
                    split_weights(se_w[:, :], se_wh[:, :], se_wl[:, :]).then_inc(front_lo, 1)
                if at(i, 0):
                    dve.wait_ge(conv2_hi, 1)
                    split_weights(c2_w[:, :, :], c2_wh[:, :, :], c2_wl[:, :, :]).then_inc(conv2_lo, 1)
                if at(i, 1):
                    dve.wait_ge(w_back, 32)
                if has(i - 1):
                    done(dve, r_g_done, i - 1)
                    done(dve, in_mm, i - 1)
                    nc.vector.scalar_tensor_tensor(gq[:, :], ps_hn, vecs[:, BH_N:BH_N + 1], r_g[:, :],
                                                   ALU.add, ALU.mult).then_inc(gq_done, 1)
                    done(dve, gq_done, i - 1)
                    nc.vector.tensor_tensor(gw[:, :], ps_in, gq[:, :], ALU.add).then_inc(gw_done, 1)
                if has(i - 2):
                    done(dve, prob_done, i - 2)
                    nc.vector.reciprocal(rinv[:, :], rsum[:, :]).then_inc(rinv_done, 1)
                    done(dve, rinv_done, i - 2)
                    done(dve, pv_mm, i - 2)
                    for k in range(T):
                        last = nc.vector.scalar_tensor_tensor(u_att[:, k, :], ps_pv[:, k, :], rinv[:, k:k + 1],
                                                              att_b[:, :], ALU.mult, ALU.add)
                    last.then_inc(u_done, 1)
                    done(dve, u_done, i - 2)
                    nc.vector.tensor_scalar(u_min[:, :, :], u_att[:, :, :], 0.0, None,
                                            ALU.min).then_inc(u_min_done, 1)
                if has(i - 1):
                    done(dve, nn_done, i - 1)
                    nc.vector.tensor_tensor(dd[:, :], hT[nxt][:, :], nn[:, :], ALU.subtract).then_inc(dd_done, 1)
                    done(dve, dd_done, i - 1)
                    done(dve, z_g_done, i - 1)
                    nc.vector.tensor_tensor(zd[:, :], z_g[:, :], dd[:, :], ALU.mult).then_inc(zd_done, 1)
                    done(dve, zd_done, i - 1)
                    nc.vector.tensor_tensor(gru[:, :], nn[:, :], zd[:, :], ALU.add).then_inc(gru_done, 1)
                if has(i + 1):
                    done(dve, hT_done, i + 1)
                    nc.vector.tensor_copy(h_hi[nxt][:, :], hT[nxt][:, :]).then_inc(h_hi_done, 1)
                    done(dve, h_hi_done, i + 1)
                    nc.vector.tensor_tensor(h_lo[nxt][:, :], hT[nxt][:, :], h_hi[nxt][:, :].bitcast(fp32),
                                            ALU.subtract).then_inc(h_lo_done, 1)
                if has(i - 2):
                    done(dve, u_exp_done, i - 2)
                    nc.vector.scalar_tensor_tensor(u_elu[:, :, :], u_att[:, :, :], 0.0, u_exp[:, :, :],
                                                   ALU.max, ALU.add).then_inc(u_elu_done, 1)
                    done(dve, u_elu_done, i - 2)
                    moved(dve, stored, i - 4, slot)
                    nc.vector.scalar_tensor_tensor(y_out[slot][:, :, :], u_elu[:, :, :], -1.0,
                                                   x1[slot][:, :, :], ALU.add, ALU.add).then_inc(y_done, 1)
                if has(i - 1):
                    done(dve, gruT_mm, i - 1)
                    moved(dve, res_loaded, i - 1, nxt)
                    nc.vector.tensor_tensor(x1[nxt][:, :, :], ps_gruT, x_res[nxt][:, :, :],
                                            ALU.add).then_inc(x1_done, 1)
                    done(dve, x1_done, i - 1)
                    for k in range(T):
                        last = nc.vector.bn_stats(stat2[:, k, :], x1[nxt][:, k, :])
                    last.then_inc(stat2_done, 1)
                    done(dve, stat2_done, i - 1)
                    carry_wait()
                    for k in range(T):
                        last = nc.vector.bn_aggr(mv2[:, k, :], stat2[:, k, :])
                    last.then_inc(mv2_done, 1)
                if has(i + 1):
                    done(dve, c1_done, i + 1)
                    done(dve, conv2_mm, i - 1)
                    nc.vector.tensor_copy(c1_hi[nxt][:, :, PAD:PAD + N], c1[:, :, :]).then_inc(c1_hi_done, 1)
                    done(dve, msg_mm, i + 1)
                    nc.vector.tensor_tensor(msg0[:, :, :], ps_msg, msg_b[:, :].unsqueeze(1).broadcast_to([P, T, D]),
                                            ALU.add).then_inc(msg0_done, 1)
                    done(dve, msg0_done, i + 1)
                    done(dve, nmp_mm, i)
                    nc.vector.tensor_scalar(msg[:, :, :], msg0[:, :, :], 0.0, None, ALU.max).then_inc(msg_done, 1)
                if has(i - 1):
                    done(dve, rstd2_done, i - 1)
                    for k in range(T):
                        last = nc.vector.tensor_scalar(h2n[:, k, :], x1[nxt][:, k, :], mv2[:, k, 0:1],
                                                       rstd2[:, k:k + 1], ALU.subtract, ALU.mult)
                    last.then_inc(h2n_done, 1)
                    done(dve, h2n_done, i - 1)
                    done(dve, pv_mm, i - 2)
                    nc.vector.tensor_scalar(h2[:, :, :], h2n[:, :, :], 0.0, None, ALU.max).then_inc(h2_done, 1)
                if has(i + 2):
                    moved(dve, x_loaded, i + 2, slot)
                    for k in range(T):
                        last = nc.vector.bn_stats(stat1[:, k, :], x_in[slot][:, k, :])
                    last.then_inc(stat1_done, 1)
                    done(dve, stat1_done, i + 2)
                    carry_wait()
                    for k in range(T):
                        last = nc.vector.bn_aggr(mv1[:, k, :], stat1[:, k, :])
                    last.then_inc(mv1_done, 1)
                if has(i + 1):
                    done(dve, ed_done, i + 1)
                    done(dve, adjT_mm, i + 1)
                    nc.vector.tensor_tensor(a0T[:, :, :], ps_adjT, ed[:, :, :], ALU.mult).then_inc(a0T_done, 1)
                    done(dve, n_hi_done, i + 1)
                    nc.vector.tensor_tensor(n_lo[nxt][:, :], ps_nmp, n_hi[nxt][:, :].bitcast(fp32),
                                            ALU.subtract).then_inc(n_lo_done, 1)
                if has(i):
                    done(dve, conv2_mm, i)
                    done(dve, hb_done, i)
                    nc.vector.scalar_tensor_tensor(c2[:, :], ps_conv2, bn_s[:, 1:2], hb[slot][:, :],
                                                   ALU.mult, ALU.add).then_inc(c2_done, 1)
                    done(dve, c2_done, i)
                    nc.vector.tensor_scalar(c_hi[:, :], c2[:, :], 0.0, None, ALU.max).then_inc(c_hi_done, 1)
                    done(dve, c_hi_done, i)
                    nc.vector.scalar_tensor_tensor(c_lo[:, :], c2[:, :], 0.0, c_hi[:, :].bitcast(fp32),
                                                   ALU.max, ALU.subtract).then_inc(c_lo_done, 1)
                if has(i - 1):
                    done(dve, imag_row_done, i - 1)
                    for k in range(T):
                        last = nc.vector.scalar_tensor_tensor(
                            an[:, k, :], ps_a[:, k, :], imag[:, k:k + 1],
                            imag_row[:, (k // NT) * N:(k // NT + 1) * N], ALU.mult, ALU.mult)
                    last.then_inc(an_done, 1)
                    done(dve, an_done, i - 1)
                    nc.vector.scalar_tensor_tensor(score[:, :, :], an[:, :, :], SLOPE, an[:, :, :],
                                                   ALU.mult, ALU.max).then_inc(score_done, 1)
                    done(dve, score_done, i - 1)
                    done(dve, neg_done, i - 1)
                    carry_wait()
                    for k in range(T):
                        last = nc.vector.tensor_tensor_reduce(
                            out=att[:, k, :], in0=score[:, k, :], in1=neg[nxt][:, k, :], scale=1.0,
                            scalar=MASKED, op0=ALU.add, op1=ALU.max, accum_out=rmax[:, k:k + 1])
                    last.then_inc(att_done, 1)
                    done(dve, att_done, i - 1)
                    nc.vector.tensor_scalar(nmax[:, :], rmax[:, :], -1.0, None, ALU.mult).then_inc(nmax_done, 1)
                if has(i + 1):
                    moved(dve, adj_loaded, i + 1, nxt)
                    nc.vector.tensor_scalar(neg[nxt][:, :, :], adj_in[nxt][:, :, :], 0.0, MASKED,
                                            ALU.is_le, ALU.mult).then_inc(neg_done, 1)
                if has(i + 2):
                    done(dve, rstd1_done, i + 2)
                    done(dve, hT_mm, i + 1)
                    for k in range(T):
                        last = nc.vector.tensor_scalar(xn1[:, k, :], x_in[slot][:, k, :], mv1[:, k, 0:1],
                                                       rstd1[:, k:k + 1], ALU.subtract, ALU.mult)
                    last.then_inc(xn1_done, 1)

            steps(dve, step)

        @block.tensor
        def _(pe):
            def product(out, w_hi, w_lo, v_hi, v_lo, start=True, stop=True):
                nc.tensor.matmul(out, w_hi, v_hi, start=start, stop=False)
                nc.tensor.matmul(out, w_hi, v_lo, start=False, stop=False)
                return nc.tensor.matmul(out, w_lo, v_hi, start=False, stop=stop)

            def step(i, slot):
                nxt = 1 - slot

                def conv2(first, end):
                    for k in range(first, end):
                        last = product(ps_conv2, c2_wh[:, k, :], c2_wl[:, k, :],
                                       c1_hi[slot][:, :, k:k + N], c1_lo[slot][:, :, k:k + N],
                                       start=(k == 0), stop=(k == TAPS - 1))
                    if end == TAPS:
                        last.then_inc(conv2_mm, 1)

                if has(i):
                    if at(i, 0):
                        pe.wait_ge(pads_made, 1)
                        pe.wait_ge(conv2_lo, 1)
                    done(pe, c1_lo_done, i)
                    done(pe, c2_done, i - 1)
                    conv2(0, 3)
                if has(i - 2):
                    done(pe, probT_done, i - 2)
                    done(pe, n_lo_done, i)
                    for k in range(T):
                        for m in range(NT):
                            t = k // NT * NT + m
                            last = nc.tensor.matmul(ps_pv[:, k, :], probT[:, t, (k % NT) * P:(k % NT + 1) * P],
                                                    h2[:, t, :], start=(m == 0), stop=(m == NT - 1))
                    last.then_inc(pv_mm, 1)
                if has(i):
                    conv2(3, 7)
                if has(i + 1):
                    if at(i, -1):
                        pe.wait_ge(ident_made, 1)
                        pe.wait_ge(front_lo, 1)
                    done(pe, xn1_done, i + 1)
                    done(pe, probT_done, i - 2)
                    done(pe, dist_in, i)
                    for k in range(T):
                        last = nc.tensor.transpose(ps_hT[:, k * P:(k + 1) * P], xn1[:, k, :], ident[:, :])
                    last.then_inc(hT_mm, 1)
                if has(i):
                    conv2(7, 9)
                if has(i - 1):
                    done(pe, gru_done, i - 1)
                    done(pe, probT_done, i - 2)
                    done(pe, msg0_done, i)
                    for k in range(T):
                        last = nc.tensor.transpose(ps_gruT[:, k, :], gru[:, k * P:(k + 1) * P], ident[:, :])
                    last.then_inc(gruT_mm, 1)
                if has(i + 1):
                    done(pe, h_lo_done, i + 1)
                    done(pe, u_done, i - 2)
                    done(pe, n_lo_done, i)
                    product(ps_conv1, c1_wh[:, :], c1_wl[:, :], h_hi[nxt][:, :],
                            h_lo[nxt][:, :]).then_inc(conv1_mm, 1)
                    done(pe, hT_done, i + 1)
                    product(ps_se, se_wh[:, :], se_wl[:, :], h_hi[nxt][:, :],
                            h_lo[nxt][:, :]).then_inc(se_mm, 1)
                    done(pe, x1_done, i - 1)
                    done(pe, msg0_done, i)
                    for k in range(T):
                        last = product(ps_msg[:, k, :], h_hi[nxt][:, k * P:(k + 1) * P],
                                       h_lo[nxt][:, k * P:(k + 1) * P], msg_wh[:, :], msg_wl[:, :])
                    last.then_inc(msg_mm, 1)
                if has(i):
                    conv2(9, 12)
                if has(i + 1):
                    moved(pe, adj_loaded, i + 1, nxt)
                    done(pe, z_t_done, i - 1)
                    done(pe, a0T_done, i)
                    for k in range(T):
                        for m in range(NT):
                            last = nc.tensor.transpose(
                                ps_adjT[:, k // NT * NT + m, (k % NT) * P:(k % NT + 1) * P],
                                adj_in[nxt][:, k, m * P:(m + 1) * P], ident[:, :])
                    last.then_inc(adjT_mm, 1)
                    done(pe, dist_sq, i + 1)
                    done(pe, gw_done, i - 1)
                    done(pe, ed_done, i)
                    for k in range(T):
                        g = k // NT
                        last = nc.tensor.matmul(ps_dist[:, k, :], dl[:, k * P:(k + 1) * P],
                                                dr[:, g * N:(g + 1) * N], start=True, stop=True)
                    last.then_inc(dist_mm, 1)
                if has(i - 1):
                    done(pe, h2_done, i - 1)
                    done(pe, probT_done, i - 2)
                    done(pe, dist_in, i + 1)
                    for k in range(T):
                        last = nc.tensor.transpose(ps_h2T[:, k * P:(k + 1) * P], h2[:, k, :], ident[:, :])
                    last.then_inc(h2T_mm, 1)
                if has(i):
                    conv2(12, 13)
                if has(i - 1):
                    if at(i, 1):
                        pe.wait_ge(w_back, 32)
                    done(pe, h2T_done, i - 1)
                    done(pe, c1_done, i + 1)
                    done(pe, u_done, i - 2)
                    nc.tensor.matmul(ps_xp, a_w[:, :], h2T[:, :], start=True, stop=True).then_inc(xp_mm, 1)
                if has(i):
                    conv2(13, 14)
                if has(i - 1):
                    done(pe, xp_done, i - 1)
                    done(pe, msg0_done, i + 1)
                    for k in range(T):
                        g = k // NT
                        last = nc.tensor.matmul(ps_a[:, k, :], xpT[:, k * P:(k + 1) * P],
                                                xpT[:, g * N:(g + 1) * N], start=True, stop=True)
                    last.then_inc(a_mm, 1)
                if has(i + 1):
                    done(pe, a0T_done, i + 1)
                    done(pe, msg_done, i + 1)
                    done(pe, xp_done, i - 1)
                    done(pe, c1_done, i + 1)
                    for g in range(G):
                        for m in range(NT):
                            last = nc.tensor.matmul(ps_nmp[:, g * N:(g + 1) * N], msg[:, g * NT + m, :],
                                                    a0T[:, g * NT + m, :], start=(m == 0), stop=(m == NT - 1))
                    last.then_inc(nmp_mm, 1)
                if has(i):
                    conv2(14, TAPS)
                if has(i - 1):
                    done(pe, imag_done, i - 1)
                    done(pe, a0T_done, i + 1)
                    done(pe, z_t_done, i - 1)
                    for k in range(T):
                        last = nc.tensor.transpose(ps_imag[:, k * P:(k + 1) * P],
                                                   imag[:, k:k + 1].broadcast_to([P, P]), ident[:, :])
                    last.then_inc(imag_mm, 1)
                if has(i):
                    if at(i, 0):
                        pe.wait_ge(gate_lo, 1)

                    def gate(out, source, part, v_hi, v_lo, start, stop):
                        cols = slice(part * D, (part + 1) * D)
                        return product(out, g_wh[:, source, cols], g_wl[:, source, cols], v_hi, v_lo,
                                       start, stop)

                    h = h_hi[slot][:, :], h_lo[slot][:, :]
                    ne = n_hi[slot][:, :], n_lo[slot][:, :]
                    co = c_hi[:, :], c_lo[:, :]
                    done(pe, r_t_done, i - 1)
                    done(pe, a0T_done, i + 1)
                    gate(ps_r, 2, 0, *h, True, False)
                    gate(ps_r, 1, 0, *ne, False, False)
                    done(pe, gw_done, i - 1)
                    done(pe, ed_done, i + 1)
                    gate(ps_hn, 2, 2, *h, True, True)
                    gate(ps_in, 1, 2, *ne, True, False)
                    done(pe, imag_row_done, i - 1)
                    done(pe, z_t_done, i - 1)
                    gate(ps_z, 2, 1, *h, True, False)
                    gate(ps_z, 1, 1, *ne, False, False)
                    done(pe, c_lo_done, i)
                    gate(ps_r, 0, 0, *co, False, True).then_inc(r_mm, 1)
                    gate(ps_z, 0, 1, *co, False, True).then_inc(z_mm, 1)
                    gate(ps_in, 0, 2, *co, False, True).then_inc(in_mm, 1)
                if has(i - 1):
                    done(pe, prob_done, i - 1)
                    done(pe, an_done, i - 1)
                    for k in range(T):
                        for m in range(NT):
                            last = nc.tensor.transpose(
                                ps_probT[:, k // NT * NT + m, (k % NT) * P:(k % NT + 1) * P],
                                prob[:, k, m * P:(m + 1) * P], ident[:, :])
                    last.then_inc(probT_mm, 1)

            steps(pe, step)


def kernel(**inputs):
    import numpy as np
    import concourse.bacc as bacc
    from concourse.bass_utils import run_bass_kernel_spmd

    def a(name):
        return np.asarray(inputs[name])

    def g(name):
        return a("L0_gnn_" + name)

    rows = [g(f"bn{n}_{v}") for n in (1, 2) for v in "gbmv"]
    rows += list(g("b_ih").reshape(3, D)) + list(g("b_hh").reshape(3, D))
    arrays = {
        "x": a("x"),
        "adj": a("adj"),
        "vec": np.stack(rows, axis=1),
        "w_se": g("w_se").T,
        "b_se": g("b_se").reshape(S, 1),
        "w_c1": g("conv1_w")[:, :, 0].T,
        "w_c2": g("conv2_w").transpose(1, 2, 0),
        "w_msg": g("w_msg").T,
        "b_msg": g("b_msg").reshape(1, D),
        "w_ih": g("w_ih").reshape(3 * D, 2, D).transpose(2, 1, 0),
        "w_hh": g("w_hh").T,
        "w_a": a("L1_gnn_W_a"),
        "bias": a("L1_gnn_bias").reshape(1, D),
    }
    arrays = {f"{n}_dram": np.ascontiguousarray(v) for n, v in arrays.items()}
    nc = bacc.Bacc("TRN2", target_bir_lowering=False, num_devices=1)
    args = [nc.dram_tensor(n, v.shape, mybir.dt.from_np(v.dtype), kind="ExternalInput").ap()
            for n, v in arrays.items()]
    out = nc.dram_tensor("out_dram", (B, N, D), mybir.dt.float32, kind="ExternalOutput").ap()
    build(nc, *args, out)
    r = run_bass_kernel_spmd(nc, [arrays], core_ids=[0])
    return r.results[0]["out_dram"]
```

```python
import concourse.bass as bass
from concourse import mybir
from contextlib import ExitStack

B, N, D = 32, 256, 128
P = 128
G = 2
PAIRS = B // G
NT = N // P
T = G * NT
C = G * N
TAPS = 17
PAD = TAPS // 2
S = 3
SE = D + S
Q = 32
LR = 4 * S + 4
LN_EPS = 1e-5
BN_EPS = 1e-5
SLOPE = -0.2
MASKED = -3.0e38

(BN1_G, BN1_B, BN1_M, BN1_V, BN2_G, BN2_B, BN2_M, BN2_V,
 BI_R, BI_Z, BI_N, BH_R, BH_Z, BH_N) = range(14)
NVEC = 14


def build(nc, x, adj, vec, b_se, w_c1, w_c2, w_msg, b_msg, w_ih, w_hh, w_a, bias, out):
    fp32 = mybir.dt.float32
    f32r = mybir.dt.float32r
    ALU = mybir.AluOpType
    ACT = mybir.ActivationFunctionType

    x_v = x.rearrange("(a g) (t p) d -> a p (g t) d", g=G, p=P)
    adj_v = adj.rearrange("(a g) (t p) m -> a p (g t) m", g=G, p=P)
    out_v = out.rearrange("(a g) (t p) d -> a p (g t) d", g=G, p=P)

    ctx = ExitStack()
    with ctx:
        def sb(name, shape, dt=fp32):
            return ctx.enter_context(nc.sbuf_tensor(name, shape, dt))

        def two(name, shape, dt=fp32):
            return [sb(f"{name}{s}", shape, dt) for s in range(2)]

        def sem(name):
            return ctx.enter_context(nc.semaphore(name))

        ident = sb("ident", [P, P])
        vecs = sb("vecs", [P, NVEC])
        c1_w, c1_wh, c1_wl = sb("c1_w", [P, D]), sb("c1_wh", [P, D], f32r), sb("c1_wl", [P, D], f32r)
        c2_wh, c2_wl = (sb(n, [P, TAPS, D], f32r) for n in ("c2_wh", "c2_wl"))
        msg_w = sb("msg_w", [P, SE])
        g_w, g_wh, g_wl = (sb(n, [P, 3, 3 * D], dt) for n, dt in
                           (("g_w", fp32), ("g_wh", f32r), ("g_wl", f32r)))
        a_w = sb("a_w", [P, D])
        msg_b = sb("msg_b", [P, D])
        att_b = sb("att_b", [P, D])
        half = sb("half", [P, T])
        bn_s = sb("bn_s", [P, 2])
        bn_b = sb("bn_b", [P, 2])
        bn_t = sb("bn_t", [P, 2])
        gate_b = sb("gate_b", [P, 2])
        gate_t = sb("gate_t", [P, 2])
        se_b = sb("se_b", [P, S])
        eps = sb("eps", [P, T])
        tick_v, tick_p = sb("tick_v", [P, 1]), sb("tick_p", [P, 2])

        x_in = two("x_in", [P, T, D])
        adj_in = two("adj_in", [P, T, N])
        stat1, mv1 = sb("stat1", [P, T, 6]), sb("mv1", [P, T, 2])
        var1, rstd1 = sb("var1", [P, T]), sb("rstd1", [P, T])
        xn1 = sb("xn1", [P, T, D])
        hT = two("hT", [P, C])
        h_hi, h_lo = two("h_hi", [P, C], f32r), two("h_lo", [P, C], f32r)
        hb = two("hb", [P, C])
        c1 = sb("c1", [P, G, N])
        c1_hi = two("c1_hi", [P, G, N + 2 * PAD], f32r)
        c1_lo = two("c1_lo", [P, G, N + 2 * PAD], f32r)
        emb, emb_sq, emb_q = sb("emb", [P, T, S]), sb("emb_sq", [P, T, S]), sb("emb_q", [P, T, 1])
        lr = sb("lr", [P, T, P // Q, Q])
        dl, dr = sb("dl", [P, C], f32r), sb("dr", [P, C], f32r)
        msg0 = sb("msg0", [P, T, D])
        msg_hi, msg_lo = sb("msg_hi", [P, T, D], f32r), sb("msg_lo", [P, T, D], f32r)
        ed = sb("ed", [P, T, N])
        a0T = sb("a0T", [P, T, N])
        a0T_hi, a0T_lo = sb("a0T_hi", [P, T, N], f32r), sb("a0T_lo", [P, T, N], f32r)
        n_hi, n_lo = two("n_hi", [P, C], f32r), two("n_lo", [P, C], f32r)
        neg = two("neg", [P, T, N])
        c2 = sb("c2", [P, C])
        c_hi, c_lo = sb("c_hi", [P, C], f32r), sb("c_lo", [P, C], f32r)
        r_t, z_t, r_g, z_g = sb("r_t", [P, C]), sb("z_t", [P, C]), sb("r_g", [P, C]), sb("z_g", [P, C])
        gq, gw, nn = sb("gq", [P, C]), sb("gw", [P, C]), sb("nn", [P, C])
        dd, zd, gru = sb("dd", [P, C]), sb("zd", [P, C]), sb("gru", [P, C])
        x_res = two("x_res", [P, T, D])
        x1 = two("x1", [P, T, D])
        stat2, mv2 = sb("stat2", [P, T, 6]), sb("mv2", [P, T, 2])
        var2, rstd2 = sb("var2", [P, T]), sb("rstd2", [P, T])
        h2n, h2 = sb("h2n", [P, T, D]), two("h2", [P, T, D])
        h2T = sb("h2T", [P, C])
        xp_hi, xp_lo = sb("xp_hi", [P, C], f32r), sb("xp_lo", [P, C], f32r)
        mag2, imag = sb("mag2", [P, T]), sb("imag", [P, T])
        imag_row = sb("imag_row", [P, C])
        shared = sb("shared", [P, TAPS * D])
        c2_w = shared[:, :].rearrange("p (k d) -> p k d", k=TAPS)
        an, score = (shared[:, s * T * N:(s + 1) * T * N].rearrange("p (t m) -> p t m", t=T) for s in range(2))
        att, prob = (sb(n, [P, T, N]) for n in ("att", "prob"))
        rmax, nmax = sb("rmax", [P, T]), sb("nmax", [P, T])
        rsum, rinv = sb("rsum", [P, T]), sb("rinv", [P, T])
        probT = sb("probT", [P, T, N])
        u_att, u_pos, u_exp, u_elu = (sb(n, [P, T, D]) for n in ("u_att", "u_pos", "u_exp", "u_elu"))
        y_out = two("y_out", [P, T, D])

        bank = ctx.enter_context(nc.psum_tensor("bank", [P, 8, 512], fp32))

        def tiles(b):
            return bank[:, b, :].rearrange("p (t d) -> p t d", t=T)

        def rows(b, n=1):
            return bank[:, b:b + n, :].rearrange("p a (t m) -> p (a t) m", t=NT)

        ps_conv2 = bank[:, 0, :]
        ps_adjT = rows(1, 2)
        ps_r, ps_z, ps_hn, ps_in = (bank[:, b, :] for b in (1, 2, 3, 4))
        ps_imag = bank[:, 2, :]
        ps_dist = rows(3, 2)
        ps_conv1 = bank[:, 3, :]
        ps_msg = bank[:, 4:6, 0:NT * SE].rearrange("p g (t e) -> p g t e", t=NT)
        ps_xp, ps_nmp = bank[:, 5, :], bank[:, 5, :]
        ps_pv = tiles(6)
        ps_hT, ps_h2T = bank[:, 6, :], bank[:, 6, :]
        ps_gruT = tiles(7)
        ps_lrT = bank[:, 7, :]
        ps_a, ps_probT = rows(6, 2), rows(1, 2)

        x_loaded = [sem("x_loaded0"), sem("x_loaded1")]
        adj_loaded = [sem("adj_loaded0"), sem("adj_loaded1")]
        res_loaded = [sem("res_loaded0"), sem("res_loaded1")]
        stored = [sem("stored0"), sem("stored1")]
        w_vec, w_front, w_conv2, w_gate, w_back, w_seb = (
            sem(n) for n in ("w_vec", "w_front", "w_conv2", "w_gate", "w_back", "w_seb"))
        ident_made, front_hi, front_lo = (
            sem(n) for n in ("ident_made", "front_hi", "front_lo"))
        conv2_hi, conv2_lo, gate_hi, gate_lo, pads_made = (
            sem(n) for n in ("conv2_hi", "conv2_lo", "gate_hi", "gate_lo", "pads_made"))
        setup, consts_made, dist_consts = (
            sem(n) for n in ("setup", "consts_made", "dist_consts"))
        stat1_done, mv1_done, var1_done, rstd1_done, xn1_done = (
            sem(n) for n in ("stat1_done", "mv1_done", "var1_done", "rstd1_done", "xn1_done"))
        hT_mm, hT_done, h_hi_done, h_lo_done, hb_done = (
            sem(n) for n in ("hT_mm", "hT_done", "h_hi_done", "h_lo_done", "hb_done"))
        conv1_mm, c1_done, c1_hi_done, c1_lo_done = (
            sem(n) for n in ("conv1_mm", "c1_done", "c1_hi_done", "c1_lo_done"))
        emb_done, emb_hi_done, emb_q_done, q_hi_done, lr_done, lrT_mm, lrT_done = (
            sem(n) for n in ("emb_done", "emb_hi_done", "emb_q_done", "q_hi_done", "lr_done", "lrT_mm", "lrT_done"))
        msg_mm, msg0_done, msg_hi_done, msg_lo_done = (
            sem(n) for n in ("msg_mm", "msg0_done", "msg_hi_done", "msg_lo_done"))
        adjT_mm, dist_mm, ed_done, a0T_done, a0T_hi_done, a0T_lo_done = (
            sem(n) for n in ("adjT_mm", "dist_mm", "ed_done", "a0T_done", "a0T_hi_done", "a0T_lo_done"))
        nmp_mm, n_hi_done, n_lo_done, neg_done = (sem(n) for n in ("nmp_mm", "n_hi_done", "n_lo_done", "neg_done"))
        conv2_mm, c2_done, c_hi_done, c_lo_done = (sem(n) for n in ("conv2_mm", "c2_done", "c_hi_done", "c_lo_done"))
        r_mm, z_mm, in_mm = sem("r_mm"), sem("z_mm"), sem("in_mm")
        r_t_done, z_t_done, r_g_done, z_g_done = (sem(n) for n in ("r_t_done", "z_t_done", "r_g_done", "z_g_done"))
        gq_done, gw_done, nn_done, dd_done, zd_done, gru_done = (
            sem(n) for n in ("gq_done", "gw_done", "nn_done", "dd_done", "zd_done", "gru_done"))
        gruT_mm, x1_done, stat2_done, mv2_done, var2_done, rstd2_done = (
            sem(n) for n in ("gruT_mm", "x1_done", "stat2_done", "mv2_done", "var2_done", "rstd2_done"))
        h2n_done, h2_done, h2T_mm, h2T_done, xp_mm, xp_hi_done, xp_lo_done = (
            sem(n) for n in ("h2n_done", "h2_done", "h2T_mm", "h2T_done", "xp_mm", "xp_hi_done", "xp_lo_done"))
        a_mm, mag2_done, imag_done, imag_mm, imag_row_done = (
            sem(n) for n in ("a_mm", "mag2_done", "imag_done", "imag_mm", "imag_row_done"))
        an_done, score_done, att_done, nmax_done, prob_done, rinv_done = (
            sem(n) for n in ("an_done", "score_done", "att_done", "nmax_done", "prob_done", "rinv_done"))
        probT_mm, probT_done, pv_mm = sem("probT_mm"), sem("probT_done"), sem("pv_mm")
        u_done, u_pos_done, u_exp_done, u_elu_done, y_done = (
            sem(n) for n in ("u_done", "u_pos_done", "u_exp_done", "u_elu_done", "y_done"))

        def done(eng, s, k):
            if not isinstance(k, int) or 0 <= k < PAIRS:
                eng.wait_ge(s, k + 1)

        def half_done(eng, s, k, g):
            if not isinstance(k, int) or 0 <= k < PAIRS:
                eng.wait_ge(s, G * k + (g + 1))

        def moved(eng, s, k, slot):
            if not isinstance(k, int) or 0 <= k < PAIRS:
                eng.wait_ge(s[slot], 8 * k + (8 if slot else 16))

        def steps(eng, step):
            for i in range(-2, 2):
                step(i, i % 2)
            with eng.Fori(1, PAIRS // 2 - 1) as j:
                step(2 * j, 0)
                step(2 * j + 1, 1)
            for i in range(PAIRS - 2, PAIRS + 2):
                step(i, i % 2)

        def at(i, first):
            return isinstance(i, int) and i == first

        def has(k):
            return not isinstance(k, int) or 0 <= k < PAIRS

        block = ctx.enter_context(nc.Block())

        @block.sync
        def _(sp):
            def step(i, slot):
                if has(i + 2):
                    done(sp, xn1_done, i)
                    sp.dma_start(x_in[slot][:, :, :], x_v[i + 2, :, :, :]).then_inc(x_loaded[slot], 16)
                    done(sp, neg_done, i)
                    done(sp, adjT_mm, i)
                    sp.dma_start(adj_in[slot][:, :, :], adj_v[i + 2, :, :, :]).then_inc(adj_loaded[slot], 16)
                if has(i):
                    done(sp, x1_done, i - 2)
                    sp.dma_start(x_res[slot][:, :, :], x_v[i, :, :, :]).then_inc(res_loaded[slot], 16)
                if has(i - 2):
                    done(sp, y_done, i - 2)
                    sp.dma_start(out_v[i - 2, :, :, :], y_out[slot][:, :, :]).then_inc(stored[slot], 16)

            steps(sp, step)
            for slot in range(2):
                sp.wait_ge(stored[slot], 16 * (PAIRS // 2 + 1))

        @block.gpsimd
        def _(pool):
            pool.memset(ident[:, :], 0.0).then_inc(setup, 1)
            pool.wait_ge(setup, 1)
            pool.affine_select(out=ident[:, :], in_=ident[:, :], compare_op=ALU.not_equal, fill=1.0,
                               base=0, pattern=[[-1, P]], channel_multiplier=1).then_inc(ident_made, 1)
            pool.memset(eps[:, :], LN_EPS)
            for slot in range(2):
                pool.memset(tick_p[:, slot:slot + 1], 0.0).then_inc(stored[slot], 16)
            pool.memset(half[:, :], -0.5).then_inc(setup, 1)
            pool.wait_ge(w_vec, 16)
            pool.wait_ge(setup, 2)
            pool.tensor_scalar(bn_t[:, :], vecs[:, BN1_V:BN2_V + 1:BN2_V - BN1_V], 1.0, BN_EPS,
                               ALU.mult, ALU.add).then_inc(setup, 1)
            pool.wait_ge(setup, 3)
            pool.tensor_tensor(bn_s[:, :], bn_t[:, :], half[:, 0:2], ALU.pow).then_inc(setup, 1)
            pool.wait_ge(setup, 4)
            pool.tensor_tensor(bn_t[:, :], bn_s[:, :], vecs[:, BN1_G:BN2_G + 1:BN2_G - BN1_G],
                               ALU.mult).then_inc(setup, 1)
            pool.wait_ge(setup, 5)
            pool.tensor_copy(bn_s[:, :], bn_t[:, :])
            pool.tensor_tensor(bn_b[:, :], bn_t[:, :], vecs[:, BN1_M:BN2_M + 1:BN2_M - BN1_M],
                               ALU.mult).then_inc(setup, 1)
            pool.wait_ge(setup, 6)
            pool.tensor_tensor(bn_t[:, :], vecs[:, BN1_B:BN2_B + 1:BN2_B - BN1_B], bn_b[:, :],
                               ALU.subtract).then_inc(setup, 1)
            pool.wait_ge(setup, 7)
            pool.tensor_copy(bn_b[:, :], bn_t[:, :])
            pool.tensor_tensor(gate_t[:, :], vecs[:, BI_R:BI_Z + 1], vecs[:, BH_R:BH_Z + 1],
                               ALU.add).then_inc(setup, 1)
            pool.wait_ge(setup, 8)
            pool.tensor_scalar(gate_b[:, :], gate_t[:, :], 0.5, 0.0, ALU.mult, ALU.add).then_inc(consts_made, 1)
            for slot in range(2):
                for half_ in (c1_hi[slot], c1_lo[slot]):
                    pool.memset(half_[:, :, 0:PAD].bitcast(fp32), 0.0)
                    last = pool.memset(half_[:, :, PAD + N:PAD + N + PAD].bitcast(fp32), 0.0)
            last.then_inc(pads_made, 1)

            def step(i, slot):
                nxt = 1 - slot
                if at(i, 0):
                    pool.wait_ge(gate_hi, 1)
                    pool.tensor_tensor(g_wl[:, :, :], g_w[:, :, :], g_wh[:, :, :].bitcast(fp32),
                                       ALU.subtract).then_inc(gate_lo, 1)
                    pool.wait_ge(gate_lo, 1)
                if has(i + 2):
                    done(pool, mv1_done, i + 2)
                    pool.tensor_tensor(var1[:, :], mv1[:, :, 1], eps[:, :], ALU.add).then_inc(var1_done, 1)
                    done(pool, var1_done, i + 2)
                    pool.tensor_tensor(rstd1[:, :], var1[:, :], half[:, :], ALU.pow).then_inc(rstd1_done, 1)
                if has(i - 1):
                    done(pool, mv2_done, i - 1)
                    pool.tensor_tensor(var2[:, :], mv2[:, :, 1], eps[:, :], ALU.add).then_inc(var2_done, 1)
                    done(pool, var2_done, i - 1)
                    pool.tensor_tensor(rstd2[:, :], var2[:, :], half[:, :], ALU.pow).then_inc(rstd2_done, 1)
                if has(i + 1):
                    done(pool, c1_hi_done, i + 1)
                    pool.tensor_tensor(c1_lo[nxt][:, :, PAD:PAD + N], c1[:, :, :],
                                       c1_hi[nxt][:, :, PAD:PAD + N].bitcast(fp32),
                                       ALU.subtract).then_inc(c1_lo_done, 1)
                    pool.tensor_scalar(hb[nxt][:, :], hT[nxt][:, :], 1.0, bn_b[:, 1:2],
                                       ALU.mult, ALU.add).then_inc(hb_done, 1)
                if has(i + 1):
                    done(pool, a0T_hi_done, i + 1)
                    done(pool, nmp_mm, i)
                    pool.tensor_tensor(a0T_lo[:, :, :], a0T[:, :, :], a0T_hi[:, :, :].bitcast(fp32),
                                       ALU.subtract).then_inc(a0T_lo_done, 1)
                if has(i - 1):
                    done(pool, mag2_done, i - 1)
                    pool.tensor_tensor(imag[:, :], mag2[:, :], half[:, :], ALU.pow).then_inc(imag_done, 1)
                if has(i):
                    done(pool, r_t_done, i)
                    pool.tensor_tensor(tick_p[:, 0:1], half[:, 0:1], half[:, 0:1], ALU.mult)
                    pool.tensor_scalar(r_g[:, :], r_t[:, :], 0.5, 0.5, ALU.mult, ALU.add).then_inc(r_g_done, 1)
                    done(pool, z_t_done, i)
                    pool.tensor_tensor(tick_p[:, 1:2], half[:, 0:1], half[:, 0:1], ALU.mult)
                    pool.tensor_scalar(z_g[:, :], z_t[:, :], 0.5, 0.5, ALU.mult, ALU.add).then_inc(z_g_done, 1)

            steps(pool, step)

        @block.scalar
        def _(act):
            act.dma_start(vecs[:, :], vec).then_inc(w_vec, 16)
            act.dma_start(c1_w[:, :], w_c1).then_inc(w_front, 16)
            act.dma_start(msg_w[:, :], w_msg).then_inc(w_front, 16)
            act.dma_start(se_b[:, :], b_se.broadcast_to([P, S])).then_inc(w_front, 16)
            act.dma_start(msg_b[:, :], b_msg.broadcast_to([P, D])).then_inc(w_front, 16)
            act.dma_start(c2_w[:, :, :], w_c2).then_inc(w_conv2, 16)
            act.dma_start(g_w[:, 0:2, :], w_ih).then_inc(w_gate, 16)
            act.dma_start(g_w[:, 2, :], w_hh).then_inc(w_gate, 16)
            act.dma_start(a_w[:, :], w_a).then_inc(w_back, 16)
            act.dma_start(att_b[:, :], bias.broadcast_to([P, D])).then_inc(w_back, 16)
            def step(i, slot):
                nxt = 1 - slot
                if at(i, -1):
                    act.wait_ge(w_conv2, 16)
                    act.activation(c2_wh[:, :, :], c2_w[:, :, :], ACT.Copy).then_inc(conv2_hi, 1)
                if at(i, 0):
                    act.wait_ge(w_gate, 32)
                    act.activation(g_wh[:, :, :], g_w[:, :, :], ACT.Copy).then_inc(gate_hi, 1)
                if has(i - 1):
                    done(act, gw_done, i - 1)
                    act.activation(nn[:, :], gw[:, :], ACT.Tanh,
                                   bias=vecs[:, BI_N:BI_N + 1]).then_inc(nn_done, 1)
                if has(i + 1):
                    done(act, hT_mm, i + 1)
                    done(act, dd_done, i - 1)
                    done(act, hb_done, i - 1)
                    done(act, h_lo_done, i - 1)
                    act.activation(hT[nxt][:, :], ps_hT, ACT.Relu).then_inc(hT_done, 1)
                    done(act, msg_mm, i - 1)
                    done(act, in_mm, i - 1)
                    act.activation(h_hi[nxt][:, :], ps_hT, ACT.Relu).then_inc(h_hi_done, 1)
                if has(i - 2):
                    done(act, probT_mm, i - 2)
                    act.activation(probT[:, :, :], ps_probT, ACT.Copy).then_inc(probT_done, 1)
                if has(i + 1):
                    if at(i, -1):
                        act.wait_ge(consts_made, 1)
                    done(act, conv1_mm, i + 1)
                    done(act, c1_lo_done, i)
                    act.activation(c1[:, :, :], ps_conv1.rearrange("p (g n) -> p g n", g=G), ACT.Relu,
                                   scale=bn_s[:, 0:1], bias=bn_b[:, 0:1]).then_inc(c1_done, 1)
                    done(act, conv2_mm, i - 1)
                    act.activation(c1_hi[nxt][:, :, PAD:PAD + N], ps_conv1.rearrange("p (g n) -> p g n", g=G),
                                   ACT.Relu, scale=bn_s[:, 0:1], bias=bn_b[:, 0:1]).then_inc(c1_hi_done, 1)
                    done(act, lrT_mm, i + 1)
                    done(act, dist_mm, i)
                    act.activation(dl[0:LR, :], ps_lrT[0:LR, :], ACT.Copy)
                    act.activation(dr[0:LR, :], ps_lrT[Q:Q + LR, :], ACT.Copy).then_inc(lrT_done, 1)
                    done(act, msg0_done, i + 1)
                    done(act, nmp_mm, i)
                    act.activation(msg_hi[:, :, :], msg0[:, :, :], ACT.Relu).then_inc(msg_hi_done, 1)
                if has(i + 1):
                    done(act, dist_mm, i + 1)
                    done(act, a0T_done, i)
                    act.activation(ed[:, :, :], ps_dist, ACT.Exp, scale=2.0).then_inc(ed_done, 1)
                if has(i - 1):
                    done(act, h2T_mm, i - 1)
                    act.activation(h2T[:, :], ps_h2T, ACT.Copy).then_inc(h2T_done, 1)
                if has(i + 1):
                    done(act, a0T_done, i + 1)
                    done(act, nmp_mm, i)
                    act.activation(a0T_hi[:, :, :], a0T[:, :, :], ACT.Copy).then_inc(a0T_hi_done, 1)
                if has(i - 2):
                    done(act, u_done, i - 2)
                    act.activation(u_exp[:, :, :], u_att[:, :, :], ACT.Exp).then_inc(u_exp_done, 1)
                if has(i - 1):
                    done(act, xp_mm, i - 1)
                    act.activation(xp_hi[:, :], ps_xp, ACT.Copy).then_inc(xp_hi_done, 1)
                if has(i - 2):
                    act.activation(u_pos[:, :, :], u_att[:, :, :], ACT.Relu).then_inc(u_pos_done, 1)
                if has(i - 1):
                    done(act, imag_done, i - 2)
                    done(act, score_done, i - 2)
                    for k in range(T):
                        if k % NT == 0:
                            half_done(act, a_mm, i - 1, k // NT)
                        last = act.activation(an[:, k, :], ps_a[:, k, :], ACT.Square,
                                              accum_out=mag2[:, k:k + 1])
                    last.then_inc(mag2_done, 1)
                if has(i + 1):
                    done(act, nmp_mm, i + 1)
                    done(act, in_mm, i - 1)
                    act.activation(n_hi[nxt][:, :], ps_nmp, ACT.Copy).then_inc(n_hi_done, 1)
                if has(i - 1):
                    done(act, imag_mm, i - 1)
                    act.activation(imag_row[:, :], ps_imag, ACT.Copy).then_inc(imag_row_done, 1)
                if has(i):
                    done(act, r_mm, i)
                    done(act, r_g_done, i - 1)
                    act.activation(r_t[:, :], ps_r, ACT.Tanh, scale=0.5,
                                   bias=gate_b[:, 0:1]).then_inc(r_t_done, 1)
                    done(act, z_mm, i)
                    act.activation(z_t[:, :], ps_z, ACT.Tanh, scale=0.5,
                                   bias=gate_b[:, 1:2]).then_inc(z_t_done, 1)
                if has(i - 1):
                    done(act, nmax_done, i - 1)
                    done(act, probT_mm, i - 2)
                    for k in range(T):
                        last = act.activation(prob[:, k, :], att[:, k, :], ACT.Exp, bias=nmax[:, k:k + 1],
                                              accum_out=rsum[:, k:k + 1])
                    last.then_inc(prob_done, 1)

            steps(act, step)

        @block.vector
        def _(dve):
            nc.vector.memset(dl[:, :].bitcast(fp32), 0.0)
            nc.vector.memset(dr[:, :].bitcast(fp32), 0.0)
            nc.vector.memset(lr[:, :, :, :], 0.0).then_inc(dist_consts, 1)
            dve.wait_ge(dist_consts, 1)
            nc.vector.memset(lr[:, :, 1, LR - 4:LR - 2], -0.5)
            nc.vector.memset(lr[:, :, 0, LR - 2:LR], -0.5).then_inc(dist_consts, 1)

            def carry_wait():
                nc.vector.memset(tick_v[:, :], 0.0)

            def split_weights(whole, hi, lo):
                return nc.vector.tensor_tensor(lo, whole, hi.bitcast(fp32), ALU.subtract)

            def step(i, slot):
                nxt = 1 - slot
                if at(i, 1):
                    dve.wait_ge(w_back, 32)
                if has(i - 1):
                    done(dve, r_g_done, i - 1)
                    done(dve, in_mm, i - 1)
                    nc.vector.scalar_tensor_tensor(gq[:, :], ps_hn, vecs[:, BH_N:BH_N + 1], r_g[:, :],
                                                   ALU.add, ALU.mult).then_inc(gq_done, 1)
                    done(dve, gq_done, i - 1)
                    nc.vector.tensor_tensor(gw[:, :], ps_in, gq[:, :], ALU.add).then_inc(gw_done, 1)
                if has(i + 2):
                    moved(dve, x_loaded, i + 2, slot)
                    for k in range(T):
                        last = nc.vector.bn_stats(stat1[:, k, :], x_in[slot][:, k, :])
                    last.then_inc(stat1_done, 1)
                    done(dve, stat1_done, i + 2)
                    carry_wait()
                    for k in range(T):
                        last = nc.vector.bn_aggr(mv1[:, k, :], stat1[:, k, :])
                    last.then_inc(mv1_done, 1)
                if has(i - 1):
                    done(dve, nn_done, i - 1)
                    nc.vector.tensor_tensor(dd[:, :], hT[nxt][:, :], nn[:, :], ALU.subtract).then_inc(dd_done, 1)
                    done(dve, dd_done, i - 1)
                    done(dve, z_g_done, i - 1)
                    nc.vector.tensor_tensor(zd[:, :], z_g[:, :], dd[:, :], ALU.mult).then_inc(zd_done, 1)
                    done(dve, zd_done, i - 1)
                    nc.vector.tensor_tensor(gru[:, :], nn[:, :], zd[:, :], ALU.add).then_inc(gru_done, 1)
                if has(i + 1):
                    done(dve, h_hi_done, i + 1)
                    nc.vector.tensor_tensor(h_lo[nxt][:, :], hT[nxt][:, :], h_hi[nxt][:, :].bitcast(fp32),
                                            ALU.subtract).then_inc(h_lo_done, 1)
                if has(i - 1):
                    done(dve, gruT_mm, i - 1)
                    moved(dve, res_loaded, i - 1, nxt)
                    nc.vector.tensor_tensor(x1[nxt][:, :, :], ps_gruT, x_res[nxt][:, :, :],
                                            ALU.add).then_inc(x1_done, 1)
                    done(dve, x1_done, i - 1)
                    for k in range(T):
                        last = nc.vector.bn_stats(stat2[:, k, :], x1[nxt][:, k, :])
                    last.then_inc(stat2_done, 1)
                    done(dve, stat2_done, i - 1)
                    carry_wait()
                    for k in range(T):
                        last = nc.vector.bn_aggr(mv2[:, k, :], stat2[:, k, :])
                    last.then_inc(mv2_done, 1)
                if has(i + 1):
                    if at(i, -1):
                        dve.wait_ge(dist_consts, 2)
                    done(dve, msg_mm, i + 1)
                    nc.vector.tensor_tensor(emb[:, :, :].rearrange("p (g t) s -> p g t s", g=G),
                                            ps_msg[:, :, :, D:D + S],
                                            se_b[:, :].unsqueeze(1).unsqueeze(1).broadcast_to([P, G, NT, S]),
                                            ALU.add).then_inc(emb_done, 1)
                    done(dve, emb_done, i + 1)
                    done(dve, lrT_mm, i)
                    emb_2 = emb[:, :, :].unsqueeze(2).broadcast_to([P, T, 2, S])
                    left = lr[:, :, 0, 0:4 * S].rearrange("p t (h c s) -> p t h c s", h=2, c=2)
                    right = lr[:, :, 1, 0:4 * S].rearrange("p t (c h s) -> p t h c s", h=2, c=2)
                    nc.vector.tensor_copy(left[:, :, 0].bitcast(f32r), emb_2)
                    nc.vector.tensor_copy(right[:, :, 0].bitcast(f32r), emb_2)
                    nc.vector.tensor_tensor(emb_sq[:, :, :], emb[:, :, :], emb[:, :, :],
                                            ALU.mult).then_inc(emb_hi_done, 1)
                    done(dve, emb_hi_done, i + 1)
                    nc.vector.tensor_tensor(left[:, :, 1], emb_2, left[:, :, 0], ALU.subtract)
                    nc.vector.tensor_tensor(right[:, :, 1], emb_2, right[:, :, 0], ALU.subtract)
                    nc.vector.reduce_sum(emb_q[:, :, :], emb_sq[:, :, :],
                                         mybir.AxisListType.X).then_inc(emb_q_done, 1)
                    done(dve, emb_q_done, i + 1)
                    sides = lr[:, :, :, :].rearrange("p t a q -> p t (a q)")
                    q_hi = sides[:, :, LR - 4:LR - 1 + Q:Q + 2]
                    q_lo = sides[:, :, LR - 3:LR + Q:Q + 2]
                    q_2 = emb_q[:, :, :].broadcast_to([P, T, 2])
                    nc.vector.tensor_copy(q_hi.bitcast(f32r), q_2).then_inc(q_hi_done, 1)
                    done(dve, q_hi_done, i + 1)
                    nc.vector.tensor_tensor(q_lo, q_2, q_hi, ALU.subtract).then_inc(lr_done, 1)
                if has(i + 1):
                    done(dve, emb_q_done, i + 1)
                    nc.vector.tensor_tensor(msg0[:, :, :].rearrange("p (g t) d -> p g t d", g=G),
                                            ps_msg[:, :, :, 0:D],
                                            msg_b[:, :].unsqueeze(1).unsqueeze(1).broadcast_to([P, G, NT, D]),
                                            ALU.add).then_inc(msg0_done, 1)
                if has(i - 1):
                    done(dve, rstd2_done, i - 1)
                    for k in range(T):
                        last = nc.vector.tensor_scalar(h2n[:, k, :], x1[nxt][:, k, :], mv2[:, k, 0:1],
                                                       rstd2[:, k:k + 1], ALU.subtract, ALU.mult)
                    last.then_inc(h2n_done, 1)
                    done(dve, h2n_done, i - 1)
                    nc.vector.tensor_scalar(h2[nxt][:, :, :], h2n[:, :, :], 0.0, None, ALU.max).then_inc(h2_done, 1)
                if has(i + 1):
                    done(dve, msg_hi_done, i + 1)
                    nc.vector.scalar_tensor_tensor(msg_lo[:, :, :], msg0[:, :, :], 0.0, msg_hi[:, :, :].bitcast(fp32),
                                                   ALU.max, ALU.subtract).then_inc(msg_lo_done, 1)
                if has(i - 2):
                    done(dve, prob_done, i - 2)
                    nc.vector.reciprocal(rinv[:, :], rsum[:, :]).then_inc(rinv_done, 1)
                    done(dve, rinv_done, i - 2)
                    done(dve, pv_mm, i - 2)
                    for k in range(T):
                        last = nc.vector.scalar_tensor_tensor(u_att[:, k, :], ps_pv[:, k, :], rinv[:, k:k + 1],
                                                              att_b[:, :], ALU.mult, ALU.add)
                    last.then_inc(u_done, 1)
                if at(i, -2):
                    dve.wait_ge(w_front, 64)
                    nc.vector.tensor_copy(c1_wh[:, :], c1_w[:, :]).then_inc(front_hi, 1)
                    dve.wait_ge(front_hi, 1)
                    split_weights(c1_w[:, :], c1_wh[:, :], c1_wl[:, :]).then_inc(front_lo, 1)
                if at(i, -1):
                    dve.wait_ge(conv2_hi, 1)
                    split_weights(c2_w[:, :, :], c2_wh[:, :, :], c2_wl[:, :, :]).then_inc(conv2_lo, 1)
                if has(i + 1):
                    done(dve, ed_done, i + 1)
                    done(dve, adjT_mm, i + 1)
                    done(dve, a0T_lo_done, i)
                    nc.vector.tensor_tensor(a0T[:, :, :], ps_adjT, ed[:, :, :], ALU.mult).then_inc(a0T_done, 1)
                if has(i - 1):
                    done(dve, xp_hi_done, i - 1)
                    for g in range(G):
                        cols = slice(g * N, (g + 1) * N)
                        nc.vector.tensor_tensor(xp_lo[:, cols], ps_xp[:, cols], xp_hi[:, cols].bitcast(fp32),
                                                ALU.subtract).then_inc(xp_lo_done, 1)
                if has(i - 2):
                    done(dve, u_pos_done, i - 2)
                    nc.vector.scalar_tensor_tensor(u_elu[:, :, :], u_exp[:, :, :], 1.0, u_pos[:, :, :],
                                                   ALU.min, ALU.add).then_inc(u_elu_done, 1)
                    done(dve, u_elu_done, i - 2)
                    moved(dve, stored, i - 2, slot)
                    nc.vector.scalar_tensor_tensor(y_out[slot][:, :, :], u_elu[:, :, :], -1.0,
                                                   x1[slot][:, :, :], ALU.add, ALU.add).then_inc(y_done, 1)
                if has(i + 2):
                    done(dve, rstd1_done, i + 2)
                    done(dve, hT_mm, i + 1)
                    for k in range(T):
                        last = nc.vector.tensor_scalar(xn1[:, k, :], x_in[slot][:, k, :], mv1[:, k, 0:1],
                                                       rstd1[:, k:k + 1], ALU.subtract, ALU.mult)
                    last.then_inc(xn1_done, 1)
                if has(i):
                    moved(dve, adj_loaded, i, slot)
                    nc.vector.tensor_scalar(neg[slot][:, :, :], adj_in[slot][:, :, :], 0.0, MASKED,
                                            ALU.is_le, ALU.mult).then_inc(neg_done, 1)
                if has(i + 1):
                    done(dve, n_hi_done, i + 1)
                    nc.vector.tensor_tensor(n_lo[nxt][:, :], ps_nmp, n_hi[nxt][:, :].bitcast(fp32),
                                            ALU.subtract).then_inc(n_lo_done, 1)
                if has(i):
                    done(dve, conv2_mm, i)
                    done(dve, hb_done, i)
                    nc.vector.scalar_tensor_tensor(c2[:, :], ps_conv2, bn_s[:, 1:2], hb[slot][:, :],
                                                   ALU.mult, ALU.add).then_inc(c2_done, 1)
                    done(dve, c2_done, i)
                    nc.vector.tensor_scalar(c_hi[:, :], c2[:, :], 0.0, None, ALU.max).then_inc(c_hi_done, 1)
                    done(dve, c_hi_done, i)
                    nc.vector.scalar_tensor_tensor(c_lo[:, :], c2[:, :], 0.0, c_hi[:, :].bitcast(fp32),
                                                   ALU.max, ALU.subtract).then_inc(c_lo_done, 1)
                if has(i - 1):
                    done(dve, imag_row_done, i - 1)
                    for k in range(T):
                        last = nc.vector.scalar_tensor_tensor(
                            an[:, k, :], ps_a[:, k, :], imag[:, k:k + 1],
                            imag_row[:, (k // NT) * N:(k // NT + 1) * N], ALU.mult, ALU.mult)
                    last.then_inc(an_done, 1)
                if has(i - 1):
                    done(dve, an_done, i - 1)
                    nc.vector.scalar_tensor_tensor(score[:, :, :], an[:, :, :], SLOPE, an[:, :, :],
                                                   ALU.mult, ALU.max).then_inc(score_done, 1)
                    done(dve, score_done, i - 1)
                    done(dve, neg_done, i - 1)
                    carry_wait()
                    for k in range(T):
                        last = nc.vector.tensor_tensor_reduce(
                            out=att[:, k, :], in0=score[:, k, :], in1=neg[nxt][:, k, :], scale=1.0,
                            scalar=MASKED, op0=ALU.add, op1=ALU.max, accum_out=rmax[:, k:k + 1])
                    last.then_inc(att_done, 1)
                    done(dve, att_done, i - 1)
                    nc.vector.tensor_scalar(nmax[:, :], rmax[:, :], -1.0, None, ALU.mult).then_inc(nmax_done, 1)

            steps(dve, step)

        @block.tensor
        def _(pe):
            def product(out, w_hi, w_lo, v_hi, v_lo, start=True, stop=True):
                nc.tensor.matmul(out, w_hi, v_hi, start=start, stop=False)
                nc.tensor.matmul(out, w_hi, v_lo, start=False, stop=False)
                return nc.tensor.matmul(out, w_lo, v_hi, start=False, stop=stop)

            def step(i, slot):
                nxt = 1 - slot

                def conv2(first, end):
                    for k in range(first, end):
                        last = product(ps_conv2, c2_wh[:, k, :], c2_wl[:, k, :],
                                       c1_hi[slot][:, :, k:k + N], c1_lo[slot][:, :, k:k + N],
                                       start=(k == 0), stop=(k == TAPS - 1))
                    if end == TAPS:
                        last.then_inc(conv2_mm, 1)

                if has(i):
                    if at(i, 0):
                        pe.wait_ge(pads_made, 1)
                        pe.wait_ge(conv2_lo, 1)
                    done(pe, c1_lo_done, i)
                    done(pe, c2_done, i - 1)
                    conv2(0, 4)
                if has(i + 1):
                    if at(i, -1):
                        pe.wait_ge(ident_made, 1)
                        pe.wait_ge(front_lo, 1)
                    done(pe, xn1_done, i + 1)
                    done(pe, an_done, i - 2)
                    done(pe, h_hi_done, i)
                    for k in range(T):
                        last = nc.tensor.transpose(ps_hT[:, k * P:(k + 1) * P], xn1[:, k, :], ident[:, :])
                    last.then_inc(hT_mm, 1)
                if has(i - 2):
                    done(pe, prob_done, i - 2)
                    done(pe, r_t_done, i - 1)
                    done(pe, z_t_done, i - 1)
                    for k in range(T):
                        for m in range(NT):
                            last = nc.tensor.transpose(
                                ps_probT[:, k // NT * NT + m, (k % NT) * P:(k % NT + 1) * P],
                                prob[:, k, m * P:(m + 1) * P], ident[:, :])
                    last.then_inc(probT_mm, 1)
                if has(i):
                    conv2(4, 7)
                if has(i - 1):
                    done(pe, gru_done, i - 1)
                    done(pe, an_done, i - 2)
                    for k in range(T):
                        last = nc.tensor.transpose(ps_gruT[:, k, :], gru[:, k * P:(k + 1) * P], ident[:, :])
                    last.then_inc(gruT_mm, 1)
                if has(i + 1):
                    done(pe, h_lo_done, i + 1)
                    done(pe, gw_done, i - 1)
                    done(pe, ed_done, i)
                    product(ps_conv1, c1_wh[:, :], c1_wl[:, :], h_hi[nxt][:, :],
                            h_lo[nxt][:, :]).then_inc(conv1_mm, 1)
                    done(pe, n_lo_done, i)
                    for k in range(T):
                        last = nc.tensor.matmul(ps_msg[:, k // NT, k % NT, :], hT[nxt][:, k * P:(k + 1) * P],
                                                msg_w[:, :], start=True, stop=True)
                    last.then_inc(msg_mm, 1)
                if has(i - 2):
                    done(pe, probT_done, i - 2)
                    done(pe, h_hi_done, i + 1)
                    done(pe, an_done, i - 2)
                    for k in range(T):
                        for m in range(NT):
                            t = k // NT * NT + m
                            rows_k = slice((k % NT) * P, (k % NT + 1) * P)
                            last = nc.tensor.matmul(ps_pv[:, k, :], probT[:, t, rows_k], h2[slot][:, t, :],
                                                    start=(m == 0), stop=(m == NT - 1))
                    last.then_inc(pv_mm, 1)
                if has(i):
                    conv2(7, 8)
                if has(i + 1):
                    done(pe, lr_done, i + 1)
                    done(pe, x1_done, i - 1)
                    for k in range(T):
                        last = nc.tensor.transpose(ps_lrT[:, k * P:(k + 1) * P],
                                                   lr[:, k, :, :].rearrange("p a q -> p (a q)"), ident[:, :])
                    last.then_inc(lrT_mm, 1)
                if has(i):
                    conv2(8, 10)
                if has(i + 1):
                    done(pe, lrT_done, i + 1)
                    done(pe, c1_hi_done, i + 1)
                    done(pe, msg0_done, i + 1)
                    for k in range(T):
                        g = k // NT
                        last = nc.tensor.matmul(ps_dist[:, k, :], dl[:, k * P:(k + 1) * P],
                                                dr[:, g * N:(g + 1) * N], start=True, stop=True)
                    last.then_inc(dist_mm, 1)
                if has(i + 1):
                    moved(pe, adj_loaded, i + 1, nxt)
                    done(pe, probT_done, i - 2)
                    done(pe, z_t_done, i - 1)
                    done(pe, a0T_done, i)
                    for k in range(T):
                        for m in range(NT):
                            last = nc.tensor.transpose(
                                ps_adjT[:, k // NT * NT + m, (k % NT) * P:(k % NT + 1) * P],
                                adj_in[nxt][:, k, m * P:(m + 1) * P], ident[:, :])
                    last.then_inc(adjT_mm, 1)
                if has(i):
                    conv2(10, 11)
                if has(i - 1):
                    done(pe, h2_done, i - 1)
                    done(pe, u_done, i - 2)
                    done(pe, an_done, i - 2)
                    done(pe, h_hi_done, i + 1)
                    for k in range(T):
                        last = nc.tensor.transpose(ps_h2T[:, k * P:(k + 1) * P], h2[nxt][:, k, :], ident[:, :])
                    last.then_inc(h2T_mm, 1)
                if has(i):
                    conv2(11, 13)
                if has(i - 1):
                    if at(i, 1):
                        pe.wait_ge(w_back, 32)
                    done(pe, h2T_done, i - 1)
                    done(pe, msg0_done, i + 1)
                    done(pe, n_lo_done, i)
                    nc.tensor.matmul(ps_xp, a_w[:, :], h2T[:, :], start=True, stop=True).then_inc(xp_mm, 1)
                if has(i):
                    conv2(13, 15)
                if has(i - 1):
                    done(pe, x1_done, i - 1)
                    done(pe, lrT_done, i + 1)
                    for g in range(G):
                        half_done(pe, xp_lo_done, i - 1, g)
                        for k in range(g * NT, (g + 1) * NT):
                            last = product(ps_a[:, k, :], xp_hi[:, k * P:(k + 1) * P],
                                           xp_lo[:, k * P:(k + 1) * P],
                                           xp_hi[:, g * N:(g + 1) * N], xp_lo[:, g * N:(g + 1) * N])
                        last.then_inc(a_mm, 1)
                if has(i + 1):
                    done(pe, a0T_lo_done, i + 1)
                    done(pe, msg_lo_done, i + 1)
                    half_done(pe, xp_lo_done, i - 1, G - 1)
                    done(pe, msg0_done, i + 1)
                    for g in range(G):
                        for m in range(NT):
                            t = g * NT + m
                            last = product(ps_nmp[:, g * N:(g + 1) * N], msg_hi[:, t, :], msg_lo[:, t, :],
                                           a0T_hi[:, t, :], a0T_lo[:, t, :],
                                           start=(m == 0), stop=(m == NT - 1))
                    last.then_inc(nmp_mm, 1)
                if has(i):
                    conv2(15, TAPS)
                if has(i - 1):
                    done(pe, imag_done, i - 1)
                    done(pe, a0T_done, i + 1)
                    done(pe, probT_done, i - 2)
                    for k in range(T):
                        last = nc.tensor.transpose(ps_imag[:, k * P:(k + 1) * P],
                                                   imag[:, k:k + 1].broadcast_to([P, P]), ident[:, :])
                    last.then_inc(imag_mm, 1)
                if has(i):
                    if at(i, 0):
                        pe.wait_ge(gate_lo, 1)

                    def gate(out, source, part, v_hi, v_lo, start, stop):
                        cols = slice(part * D, (part + 1) * D)
                        return product(out, g_wh[:, source, cols], g_wl[:, source, cols], v_hi, v_lo,
                                       start, stop)

                    h = h_hi[slot][:, :], h_lo[slot][:, :]
                    ne = n_hi[slot][:, :], n_lo[slot][:, :]
                    co = c_hi[:, :], c_lo[:, :]
                    done(pe, probT_done, i - 2)
                    done(pe, r_t_done, i - 1)
                    done(pe, a0T_done, i + 1)
                    gate(ps_r, 2, 0, *h, True, False)
                    gate(ps_r, 1, 0, *ne, False, False)
                    done(pe, gw_done, i - 1)
                    done(pe, ed_done, i + 1)
                    gate(ps_hn, 2, 2, *h, True, True)
                    gate(ps_in, 1, 2, *ne, True, False)
                    done(pe, imag_row_done, i - 1)
                    done(pe, z_t_done, i - 1)
                    gate(ps_z, 2, 1, *h, True, False)
                    gate(ps_z, 1, 1, *ne, False, False)
                    done(pe, c_lo_done, i)
                    gate(ps_r, 0, 0, *co, False, True).then_inc(r_mm, 1)
                    gate(ps_z, 0, 1, *co, False, True).then_inc(z_mm, 1)
                    gate(ps_in, 0, 2, *co, False, True).then_inc(in_mm, 1)

            steps(pe, step)


def kernel(**inputs):
    import numpy as np
    import concourse.bacc as bacc
    from concourse.bass_utils import run_bass_kernel_spmd

    def a(name):
        return np.asarray(inputs[name])

    def g(name):
        return a("L0_gnn_" + name)

    rows = [g(f"bn{n}_{v}") for n in (1, 2) for v in "gbmv"]
    rows += list(g("b_ih").reshape(3, D)) + list(g("b_hh").reshape(3, D))
    arrays = {
        "x": a("x"),
        "adj": a("adj"),
        "vec": np.stack(rows, axis=1),
        "b_se": g("b_se").reshape(1, S),
        "w_c1": g("conv1_w")[:, :, 0].T,
        "w_c2": g("conv2_w").transpose(1, 2, 0),
        "w_msg": np.concatenate([g("w_msg").T, g("w_se").T], axis=1),
        "b_msg": g("b_msg").reshape(1, D),
        "w_ih": g("w_ih").reshape(3 * D, 2, D).transpose(2, 1, 0),
        "w_hh": g("w_hh").T,
        "w_a": a("L1_gnn_W_a"),
        "bias": a("L1_gnn_bias").reshape(1, D),
    }
    arrays = {f"{n}_dram": np.ascontiguousarray(v) for n, v in arrays.items()}
    nc = bacc.Bacc("TRN2", target_bir_lowering=False, num_devices=1)
    args = [nc.dram_tensor(n, v.shape, mybir.dt.from_np(v.dtype), kind="ExternalInput").ap()
            for n, v in arrays.items()]
    out = nc.dram_tensor("out_dram", (B, N, D), mybir.dt.float32, kind="ExternalOutput").ap()
    build(nc, *args, out)
    r = run_bass_kernel_spmd(nc, [arrays], core_ids=[0])
    return r.results[0]["out_dram"]
```

```python
import concourse.bass as bass
from concourse import mybir
from contextlib import ExitStack

B, N, D = 32, 256, 128
P = 128
G = 2
PAIRS = B // G
NT = N // P
T = G * NT
C = G * N
TAPS = 17
PAD = TAPS // 2
REACH = PAD // 2
H = N // 2
EVEN, ODD = PAD + 1, PAD
S = 3
SE = D + S
Q = 32
LR = 4 * S + 4
MSG_PITCH = (512 - SE) // 2
LN_EPS = 1e-5
BN_EPS = 1e-5
SLOPE = -0.2
MASKED = -3.0e38

(BN1_G, BN1_B, BN1_M, BN1_V, BN2_G, BN2_B, BN2_M, BN2_V,
 BI_R, BI_Z, BI_N, BH_R, BH_Z, BH_N) = range(14)
NVEC = 14


def build(nc, x, adj, vec, b_se, w_c1, w_c2, w_msg, b_msg, w_ih, w_hh, w_a, bias, out):
    fp32 = mybir.dt.float32
    f32r = mybir.dt.float32r
    ALU = mybir.AluOpType
    ACT = mybir.ActivationFunctionType

    x_v = x.rearrange("(a g) (t p) d -> a p (g t) d", g=G, p=P)
    adj_v = adj.rearrange("(a g) (t p) m -> a p (g t) m", g=G, p=P)
    out_v = out.rearrange("(a g) (t p) d -> a p (g t) d", g=G, p=P)

    ctx = ExitStack()
    with ctx:
        def sb(name, shape, dt=fp32):
            return ctx.enter_context(nc.sbuf_tensor(name, shape, dt))

        def two(name, shape, dt=fp32):
            return [sb(f"{name}{s}", shape, dt) for s in range(2)]

        def sem(name):
            return ctx.enter_context(nc.semaphore(name))

        ident = sb("ident", [P, P])
        vecs = sb("vecs", [P, NVEC])
        c1_w, c1_wh, c1_wl = sb("c1_w", [P, D]), sb("c1_wh", [P, D], f32r), sb("c1_wl", [P, D], f32r)
        c2_wh, c2_wl = (sb(n, [P, TAPS, D], f32r) for n in ("c2_wh", "c2_wl"))
        c2_sh, c2_sl = (sb(n, [P, EVEN, D], f32r) for n in ("c2_sh", "c2_sl"))
        msg_w = sb("msg_w", [P, SE])
        g_wh, g_wl = (sb(n, [P, 3, 3 * D], f32r) for n in ("g_wh", "g_wl"))
        a_w = sb("a_w", [P, D])
        msg_b = sb("msg_b", [P, D])
        att_b = sb("att_b", [P, D])
        half = sb("half", [P, T])
        bn_s = sb("bn_s", [P, 2])
        bn_b = sb("bn_b", [P, 2])
        bn_t = sb("bn_t", [P, 2])
        gate_b = sb("gate_b", [P, 2])
        gate_t = sb("gate_t", [P, 2])
        se_b = sb("se_b", [P, S])
        eps = sb("eps", [P, T])
        tick_v, tick_p = sb("tick_v", [P, 1]), sb("tick_p", [P, 2])

        x_in = two("x_in", [P, T, D])
        adj_in = two("adj_in", [P, T, N])
        stat1, mv1 = sb("stat1", [P, T, 6]), sb("mv1", [P, T, 2])
        var1, rstd1 = sb("var1", [P, T]), sb("rstd1", [P, T])
        xn1 = sb("xn1", [P, T, D])
        hT = two("hT", [P, C])
        h_hi, h_lo = two("h_hi", [P, C], f32r), two("h_lo", [P, C], f32r)
        common = sb("common", [P, G, H])
        hb = sb("hb", [P, C])
        c1 = sb("c1", [P, G, 1 + N + 1])
        c1_d = sb("c1_d", [P, 2, G, H + 1])
        cv_hi, cv_lo = (two(n, [P, 3, G, REACH + H + REACH], f32r) for n in ("cv_hi", "cv_lo"))
        emb, emb_sq, emb_q = sb("emb", [P, T, S]), sb("emb_sq", [P, T, S]), sb("emb_q", [P, T, 1])
        lr = sb("lr", [P, T, P // Q, Q])
        dl, dr = sb("dl", [P, C], f32r), sb("dr", [P, C], f32r)
        msg0 = sb("msg0", [P, T, D])
        msg_hi, msg_lo = sb("msg_hi", [P, T, D], f32r), sb("msg_lo", [P, T, D], f32r)
        ed = sb("ed", [P, T, N])
        a0T = sb("a0T", [P, T, N])
        a0T_hi, a0T_lo = sb("a0T_hi", [P, T, N], f32r), sb("a0T_lo", [P, T, N], f32r)
        n_hi, n_lo = two("n_hi", [P, C], f32r), two("n_lo", [P, C], f32r)
        neg = two("neg", [P, T, N])
        c2 = sb("c2", [P, C])
        c_hi, c_lo = sb("c_hi", [P, C], f32r), sb("c_lo", [P, C], f32r)
        r_t, z_t, r_g, z_g = sb("r_t", [P, C]), sb("z_t", [P, C]), sb("r_g", [P, C]), sb("z_g", [P, C])
        gq, gw, nn = sb("gq", [P, C]), sb("gw", [P, C]), sb("nn", [P, C])
        dd, gru = sb("dd", [P, C]), sb("gru", [P, C])
        x_res = two("x_res", [P, T, D])
        x1 = two("x1", [P, T, D])
        stat2, mv2 = sb("stat2", [P, T, 6]), sb("mv2", [P, T, 2])
        var2, rstd2 = sb("var2", [P, T]), sb("rstd2", [P, T])
        h2 = two("h2", [P, T, D])
        h2T = sb("h2T", [P, C])
        xp_hi, xp_lo = sb("xp_hi", [P, C], f32r), sb("xp_lo", [P, C], f32r)
        mag2, imag = sb("mag2", [P, T]), sb("imag", [P, T])
        imag_row = sb("imag_row", [P, C])
        shared = sb("shared", [P, TAPS * D])
        c2_w = shared[:, :].rearrange("p (k d) -> p k d", k=TAPS)
        an, score = (shared[:, s * T * N:(s + 1) * T * N].rearrange("p (t m) -> p t m", t=T) for s in range(2))
        att, prob = (sb(n, [P, T, N]) for n in ("att", "prob"))
        rmax, nmax = sb("rmax", [P, T]), sb("nmax", [P, T])
        rsum, rinv = sb("rsum", [P, T]), sb("rinv", [P, T])
        probT = sb("probT", [P, T, N])
        late = sb("late", [P, 5, T, D])
        u_att, u_pos, u_exp = (late[:, n, :, :] for n in range(3))
        y_out = [late[:, 3 + s, :, :] for s in range(2)]
        raw = late[:, :, :, :].rearrange("p n t d -> p (n t d)")
        c2_s = raw[:, 0:EVEN * D].rearrange("p (k d) -> p k d", k=EVEN)
        g_w = raw[:, EVEN * D:(EVEN + 9) * D].rearrange("p (s c) -> p s c", s=3)

        bank = ctx.enter_context(nc.psum_tensor("bank", [P, 8, 512], fp32))

        def tiles(b):
            return bank[:, b, :].rearrange("p (t d) -> p t d", t=T)

        def rows(b, n=1):
            return bank[:, b:b + n, :].rearrange("p a (t m) -> p (a t) m", t=NT)

        def by_graph(g, whole, *single):
            return whole if g is None else single[g]

        ps_conv2 = bank[:, 0, :]
        ps_adjT = rows(1, 2)
        ps_r, ps_z, ps_hn, ps_in = (bank[:, b, :] for b in (1, 2, 3, 4))
        ps_dist = rows(3, 2)
        ps_conv1 = bank[:, 3, :]
        ps_msg = bank[:, 4:6, :].rearrange("p b c -> p (b c)")[:, 0:T * MSG_PITCH].rearrange(
            "p (t e) -> p t e", t=T)[:, :, 0:SE]
        ps_common = bank[:, 5, N:2 * N].rearrange("p (g j) -> p g j", g=G)
        ps_nmp = bank[:, 5, :]
        ps_hT, ps_lrT = bank[:, 6, :], bank[:, 7, :]
        ps_probT = rows(1, 2)

        def ps_gruT(g):
            return tiles(by_graph(g, 7, 7, 5))

        def ps_h2T(g):
            return bank[:, by_graph(g, 5, 0, 7), :]

        def ps_xp(g):
            return bank[:, by_graph(g, 6, 3, 4), :]

        def ps_a(k, g):
            b = by_graph(g, 6 + k // NT, 0, 7)
            return bank[:, b, k % NT * N:(k % NT + 1) * N]

        def ps_imag(g):
            return bank[:, by_graph(g, 2, 5, 6), :]

        def ps_pv(g):
            return tiles(by_graph(g, 6, 3, 4))

        def cols(g):
            return slice(0, C) if g is None else slice(g * N, (g + 1) * N)

        def tl(g):
            return slice(0, T) if g is None else slice(g * NT, (g + 1) * NT)

        def each(g):
            return range(tl(g).start, tl(g).stop)

        x_loaded = [sem("x_loaded0"), sem("x_loaded1")]
        adj_loaded = [sem("adj_loaded0"), sem("adj_loaded1")]
        res_loaded = [sem("res_loaded0"), sem("res_loaded1")]
        stored = [sem("stored0"), sem("stored1")]
        w_vec, w_conv1, w_message, w_conv2, w_gate, w_back, w_seb = (
            sem(n) for n in ("w_vec", "w_conv1", "w_message", "w_conv2", "w_gate", "w_back", "w_seb"))
        ident_made, conv1_hi, conv1_lo = (
            sem(n) for n in ("ident_made", "conv1_hi", "conv1_lo"))
        sums_made, conv2_hi, conv2_lo, gate_hi, gate_lo, pads_made = (
            sem(n) for n in ("sums_made", "conv2_hi", "conv2_lo", "gate_hi", "gate_lo", "pads_made"))
        setup, consts_made, dist_consts = (
            sem(n) for n in ("setup", "consts_made", "dist_consts"))
        stat1_done, mv1_done, var1_done, rstd1_done, xn1_done = (
            sem(n) for n in ("stat1_done", "mv1_done", "var1_done", "rstd1_done", "xn1_done"))
        hT_mm, hT_done, h_hi_done, h_lo_done, hb_done = (
            sem(n) for n in ("hT_mm", "hT_done", "h_hi_done", "h_lo_done", "hb_done"))
        conv1_mm, c1_done, c1_hi_done, c1_lo_done = (
            sem(n) for n in ("conv1_mm", "c1_done", "c1_hi_done", "c1_lo_done"))
        c1_d_done, d_hi_done, d_lo_done = (sem(n) for n in ("c1_d_done", "d_hi_done", "d_lo_done"))
        emb_done, emb_hi_done, emb_q_done, q_hi_done, lr_done, lrT_mm, lrT_done = (
            sem(n) for n in ("emb_done", "emb_hi_done", "emb_q_done", "q_hi_done", "lr_done", "lrT_mm", "lrT_done"))
        msg_mm, msg0_done, msg_hi_done, msg_lo_done = (
            sem(n) for n in ("msg_mm", "msg0_done", "msg_hi_done", "msg_lo_done"))
        adjT_mm, dist_mm, ed_done, a0T_done, a0T_hi_done, a0T_lo_done = (
            sem(n) for n in ("adjT_mm", "dist_mm", "ed_done", "a0T_done", "a0T_hi_done", "a0T_lo_done"))
        nmp_mm, n_hi_done, n_lo_done, neg_done = (sem(n) for n in ("nmp_mm", "n_hi_done", "n_lo_done", "neg_done"))
        common_mm, common_done = sem("common_mm"), sem("common_done")
        conv2_mm, c2_done, c_hi_done, c_lo_done = (sem(n) for n in ("conv2_mm", "c2_done", "c_hi_done", "c_lo_done"))
        r_mm, z_mm, in_mm = sem("r_mm"), sem("z_mm"), sem("in_mm")
        r_t_done, z_t_done, r_g_done, z_g_done = (sem(n) for n in ("r_t_done", "z_t_done", "r_g_done", "z_g_done"))
        gq_done, gw_done, nn_done, dd_done, zd_done, gru_done = (
            sem(n) for n in ("gq_done", "gw_done", "nn_done", "dd_done", "zd_done", "gru_done"))
        gruT_mm, x1_done, stat2_done, mv2_done, var2_done, rstd2_done = (
            sem(n) for n in ("gruT_mm", "x1_done", "stat2_done", "mv2_done", "var2_done", "rstd2_done"))
        h2n_done, h2_done, h2T_mm, h2T_done, xp_mm, xp_hi_done, xp_lo_done = (
            sem(n) for n in ("h2n_done", "h2_done", "h2T_mm", "h2T_done", "xp_mm", "xp_hi_done", "xp_lo_done"))
        a_mm, mag2_done, imag_done, imag_mm, imag_row_done = (
            sem(n) for n in ("a_mm", "mag2_done", "imag_done", "imag_mm", "imag_row_done"))
        an_done, score_done, att_done, nmax_done, prob_done, rinv_done = (
            sem(n) for n in ("an_done", "score_done", "att_done", "nmax_done", "prob_done", "rinv_done"))
        probT_mm, probT_done, pv_mm = sem("probT_mm"), sem("probT_done"), sem("pv_mm")
        u_done, u_pos_done, u_exp_done, u_elu_done, y_done = (
            sem(n) for n in ("u_done", "u_pos_done", "u_exp_done", "u_elu_done", "y_done"))

        LAST = PAIRS - 1
        PASSES = EVEN + ODD + EVEN

        def done(eng, s, k, g=None):
            if not isinstance(k, int) or 0 <= k < PAIRS:
                eng.wait_ge(s, k + 1 if g is None else k + 1 + g)

        def half_done(eng, s, k, g):
            if not isinstance(k, int) or 0 <= k < PAIRS:
                eng.wait_ge(s, G * k + (g + 1))

        def moved(eng, s, k, slot):
            if not isinstance(k, int) or 0 <= k < PAIRS:
                eng.wait_ge(s[slot], 8 * k + (8 if slot else 16))

        def steps(eng, step):
            step(1, 1)
            with eng.Fori(1, PAIRS // 2 - 1) as j:
                step(2 * j, 0)
                step(2 * j + 1, 1)
            step(LAST - 1, 0)

        def has(k):
            return not isinstance(k, int) or 0 <= k < PAIRS

        block = ctx.enter_context(nc.Block())

        @block.sync
        def _(sp):
            def load_x(k, s):
                done(sp, xn1_done, k - 2)
                sp.dma_start(x_in[s][:, :, :], x_v[k, :, :, :]).then_inc(x_loaded[s], 16)

            def load_adj(k, s):
                done(sp, neg_done, k - 2)
                done(sp, adjT_mm, k - 2)
                sp.dma_start(adj_in[s][:, :, :], adj_v[k, :, :, :]).then_inc(adj_loaded[s], 16)

            def load_res(k, s):
                done(sp, x1_done, k - 2)
                sp.dma_start(x_res[s][:, :, :], x_v[k, :, :, :]).then_inc(res_loaded[s], 16)

            def store(k, s, g=None):
                done(sp, y_done, k, g)
                sp.dma_start(out_v[k, :, tl(g), :], y_out[s][:, tl(g), :]).then_inc(stored[s], 16)

            def step(i, s):
                if has(i + 2):
                    load_x(i + 2, s)
                    load_adj(i + 2, s)
                load_res(i, s)
                if has(i - 2):
                    store(i - 2, s)

            load_x(0, 0)
            sp.dma_start(c1_w[:, :], w_c1).then_inc(w_conv1, 16)
            load_x(1, 1)
            sp.dma_start(msg_w[:, :], w_msg).then_inc(w_message, 16)
            load_adj(0, 0)
            load_adj(1, 1)
            load_x(2, 0)
            load_res(0, 0)
            load_adj(2, 0)
            steps(sp, step)
            load_res(LAST, 1)
            store(LAST - 2, 1)
            store(LAST - 1, 0)
            for g in range(G):
                store(LAST, 1, g)
            for s in range(2):
                sp.wait_ge(stored[s], 16 * (PAIRS // 2 + 1 + s))

        @block.gpsimd
        def _(pool):
            def carry_wait(k, c):
                if not isinstance(k, int):
                    pool.tensor_tensor(tick_p[:, c:c + 1], half[:, 0:1], half[:, 0:1], ALU.mult)

            def rstd1_(k):
                done(pool, mv1_done, k)
                pool.tensor_tensor(var1[:, :], mv1[:, :, 1], eps[:, :], ALU.add).then_inc(var1_done, 1)
                done(pool, var1_done, k)
                pool.tensor_tensor(rstd1[:, :], var1[:, :], half[:, :], ALU.pow).then_inc(rstd1_done, 1)

            def rstd2_(k, g=None):
                t = tl(g)
                done(pool, mv2_done, k, g)
                pool.tensor_tensor(var2[:, t], mv2[:, t, 1], eps[:, t], ALU.add).then_inc(var2_done, 1)
                done(pool, var2_done, k, g)
                pool.tensor_tensor(rstd2[:, t], var2[:, t], half[:, t], ALU.pow).then_inc(rstd2_done, 1)

            def c1_split(k, s):
                done(pool, c1_hi_done, k)
                pool.tensor_tensor(cv_lo[s][:, 0, :, REACH:REACH + H], c1[:, :, 1:1 + N:2],
                                   cv_hi[s][:, 0, :, REACH:REACH + H].bitcast(fp32),
                                   ALU.subtract).then_inc(c1_lo_done, 1)
                done(pool, d_lo_done, k - 1)
                pool.tensor_tensor(c1_d[:, 0, :, :], c1[:, :, 0:N + 1:2], c1[:, :, 1:N + 2:2], ALU.subtract)
                pool.tensor_tensor(c1_d[:, 1, :, 0:H], c1[:, :, 2:N + 2:2], c1[:, :, 1:N + 1:2],
                                   ALU.subtract).then_inc(c1_d_done, 1)

            def hb_(k, s):
                done(pool, common_done, k)
                done(pool, c2_done, k - 1)
                pool.tensor_tensor(hb[:, :].rearrange("p (g j q) -> p g j q", g=G, q=2),
                                   hT[s][:, :].rearrange("p (g j q) -> p g j q", g=G, q=2),
                                   common[:, :, :].unsqueeze(3).broadcast_to([P, G, H, 2]),
                                   ALU.add).then_inc(hb_done, 1)

            def d_lo_(k, s):
                done(pool, d_hi_done, k)
                pool.tensor_tensor(cv_lo[s][:, 1:3, :, REACH:REACH + H + 1], c1_d[:, :, :, :],
                                   cv_hi[s][:, 1:3, :, REACH:REACH + H + 1].bitcast(fp32),
                                   ALU.subtract).then_inc(d_lo_done, 1)

            def a0T_lo_(k):
                done(pool, a0T_hi_done, k)
                done(pool, nmp_mm, k - 1)
                pool.tensor_tensor(a0T_lo[:, :, :], a0T[:, :, :], a0T_hi[:, :, :].bitcast(fp32),
                                   ALU.subtract).then_inc(a0T_lo_done, 1)

            def imag_(k, g=None):
                t = tl(g)
                done(pool, mag2_done, k, g)
                pool.tensor_tensor(imag[:, t], mag2[:, t], half[:, t], ALU.pow).then_inc(imag_done, 1)

            def sigmoids(k, g=None):
                c = cols(g)
                done(pool, r_t_done, k, g)
                carry_wait(k, 0)
                pool.tensor_scalar(r_g[:, c], r_t[:, c], 0.5, 0.5, ALU.mult, ALU.add).then_inc(r_g_done, 1)
                done(pool, z_t_done, k, g)
                carry_wait(k, 1)
                pool.tensor_scalar(z_g[:, c], z_t[:, c], 0.5, 0.5, ALU.mult, ALU.add).then_inc(z_g_done, 1)

            def step(i, s):
                hb_(i, s)
                if has(i + 2):
                    rstd1_(i + 2)
                rstd2_(i - 1)
                if has(i + 1):
                    c1_split(i + 1, 1 - s)
                    a0T_lo_(i + 1)
                imag_(i - 1)
                if has(i + 1):
                    d_lo_(i + 1, 1 - s)
                sigmoids(i)

            pool.memset(ident[:, :], 0.0).then_inc(setup, 1)
            pool.wait_ge(setup, 1)
            pool.affine_select(out=ident[:, :], in_=ident[:, :], compare_op=ALU.not_equal, fill=1.0,
                               base=0, pattern=[[-1, P]], channel_multiplier=1).then_inc(ident_made, 1)
            pool.memset(eps[:, :], LN_EPS)
            for s in range(2):
                pool.memset(tick_p[:, s:s + 1], 0.0).then_inc(stored[s], 16)
            pool.memset(half[:, :], -0.5).then_inc(setup, 1)
            pool.wait_ge(setup, 2)
            rstd1_(0)
            pool.wait_ge(w_vec, 16)
            pool.tensor_scalar(bn_t[:, :], vecs[:, BN1_V:BN2_V + 1:BN2_V - BN1_V], 1.0, BN_EPS,
                               ALU.mult, ALU.add).then_inc(setup, 1)
            pool.wait_ge(setup, 3)
            pool.tensor_tensor(bn_s[:, :], bn_t[:, :], half[:, 0:2], ALU.pow).then_inc(setup, 1)
            pool.wait_ge(setup, 4)
            pool.tensor_tensor(bn_t[:, :], bn_s[:, :], vecs[:, BN1_G:BN2_G + 1:BN2_G - BN1_G],
                               ALU.mult).then_inc(setup, 1)
            pool.wait_ge(setup, 5)
            pool.tensor_copy(bn_s[:, :], bn_t[:, :])
            pool.tensor_tensor(bn_b[:, :], bn_t[:, :], vecs[:, BN1_M:BN2_M + 1:BN2_M - BN1_M],
                               ALU.mult).then_inc(setup, 1)
            pool.wait_ge(setup, 6)
            pool.tensor_tensor(bn_t[:, :], vecs[:, BN1_B:BN2_B + 1:BN2_B - BN1_B], bn_b[:, :],
                               ALU.subtract).then_inc(setup, 1)
            pool.wait_ge(setup, 7)
            pool.tensor_copy(bn_b[:, :], bn_t[:, :])
            pool.tensor_tensor(gate_t[:, :], vecs[:, BI_R:BI_Z + 1], vecs[:, BH_R:BH_Z + 1],
                               ALU.add).then_inc(setup, 1)
            pool.wait_ge(setup, 8)
            pool.tensor_scalar(gate_b[:, :], gate_t[:, :], 0.5, 0.0, ALU.mult, ALU.add).then_inc(consts_made, 1)
            pool.memset(c1[:, :, 0:N + 2:N + 1], 0.0)
            pool.memset(c1_d[:, 1, :, H:H + 1], 0.0)
            for s in range(2):
                for padded in (cv_hi[s], cv_lo[s]):
                    pool.memset(padded[:, :, :, 0:REACH].bitcast(fp32), 0.0)
                    last = pool.memset(padded[:, :, :, REACH + H:REACH + H + REACH].bitcast(fp32), 0.0)
            last.then_inc(pads_made, 1)
            rstd1_(1)
            c1_split(0, 0)
            d_lo_(0, 0)
            a0T_lo_(0)
            hb_(0, 0)
            pool.wait_ge(gate_hi, 1)
            pool.tensor_tensor(g_wl[:, :, :], g_w[:, :, :], g_wh[:, :, :].bitcast(fp32),
                               ALU.subtract).then_inc(gate_lo, 1)
            c1_split(1, 1)
            rstd1_(2)
            d_lo_(1, 1)
            a0T_lo_(1)
            pool.wait_ge(gate_lo, 1)
            sigmoids(0)
            steps(pool, step)
            hb_(LAST, 1)
            rstd2_(LAST - 1)
            imag_(LAST - 1)
            for g in range(G):
                sigmoids(LAST, g)
            for g in range(G):
                rstd2_(LAST, g)
            for g in range(G):
                imag_(LAST, g)

        @block.scalar
        def _(act):
            def common_(k):
                done(act, common_mm, k)
                done(act, hb_done, k - 1)
                act.activation(common[:, :, :], ps_common, ACT.Identity, scale=bn_s[:, 1:2],
                               bias=bn_b[:, 1:2]).then_inc(common_done, 1)

            def nn_(k, g=None):
                done(act, gw_done, k, g)
                act.activation(nn[:, cols(g)], gw[:, cols(g)], ACT.Tanh,
                               bias=vecs[:, BI_N:BI_N + 1]).then_inc(nn_done, 1)

            def h_rows(k, s):
                done(act, hT_mm, k)
                done(act, dd_done, k - 2)
                done(act, hb_done, k - 2)
                done(act, h_lo_done, k - 2)
                act.activation(hT[s][:, :], ps_hT, ACT.Relu).then_inc(hT_done, 1)
                done(act, in_mm, k - 2)
                act.activation(h_hi[s][:, :], ps_hT, ACT.Relu).then_inc(h_hi_done, 1)

            def probT_(k, g=None):
                done(act, probT_mm, k, g)
                act.activation(probT[:, tl(g), :], ps_probT[:, tl(g), :], ACT.Copy).then_inc(probT_done, 1)

            def c1_rows(k, s):
                done(act, conv1_mm, k)
                done(act, c1_lo_done, k - 1)
                done(act, c1_d_done, k - 1)
                ps = ps_conv1.rearrange("p (g n) -> p g n", g=G)
                act.activation(c1[:, :, 1:1 + N], ps, ACT.Relu,
                               scale=bn_s[:, 0:1], bias=bn_b[:, 0:1]).then_inc(c1_done, 1)
                done(act, conv2_mm, k - 2)
                act.activation(cv_hi[s][:, 0, :, REACH:REACH + H], ps[:, :, 0:N:2], ACT.Relu,
                               scale=bn_s[:, 0:1], bias=bn_b[:, 0:1]).then_inc(c1_hi_done, 1)

            def d_hi_(k, s):
                done(act, c1_d_done, k)
                done(act, conv2_mm, k - 2)
                act.activation(cv_hi[s][:, 1:3, :, REACH:REACH + H + 1], c1_d[:, :, :, :],
                               ACT.Copy).then_inc(d_hi_done, 1)

            def dist_operands(k):
                done(act, lrT_mm, k)
                done(act, dist_mm, k - 1)
                act.activation(dl[0:LR, :], ps_lrT[0:LR, :], ACT.Copy)
                act.activation(dr[0:LR, :], ps_lrT[Q:Q + LR, :], ACT.Copy).then_inc(lrT_done, 1)

            def msg_hi_(k):
                done(act, msg0_done, k)
                done(act, nmp_mm, k - 1)
                act.activation(msg_hi[:, :, :], msg0[:, :, :], ACT.Relu).then_inc(msg_hi_done, 1)

            def exp_dist(k):
                done(act, dist_mm, k)
                done(act, a0T_done, k - 1)
                act.activation(ed[:, :, :], ps_dist, ACT.Exp, scale=2.0).then_inc(ed_done, 1)

            def h2T_(k, g=None):
                done(act, h2T_mm, k, g)
                act.activation(h2T[:, cols(g)], ps_h2T(g)[:, cols(g)], ACT.Copy).then_inc(h2T_done, 1)

            def a0T_hi_(k):
                done(act, a0T_done, k)
                done(act, nmp_mm, k - 1)
                act.activation(a0T_hi[:, :, :], a0T[:, :, :], ACT.Copy).then_inc(a0T_hi_done, 1)

            def u_exp_(k, g=None):
                done(act, u_done, k, g)
                act.activation(u_exp[:, tl(g), :], u_att[:, tl(g), :], ACT.Exp).then_inc(u_exp_done, 1)

            def u_pos_(k, g=None):
                act.activation(u_pos[:, tl(g), :], u_att[:, tl(g), :], ACT.Relu).then_inc(u_pos_done, 1)

            def xp_hi_(k, g=None):
                done(act, xp_mm, k, g)
                act.activation(xp_hi[:, cols(g)], ps_xp(g)[:, cols(g)], ACT.Copy).then_inc(xp_hi_done, 1)

            def row_norms(k, g=None):
                done(act, imag_done, k - 1)
                done(act, score_done, k - 1)
                for t in each(g):
                    if t % NT == 0:
                        half_done(act, a_mm, k, t // NT)
                    last = act.activation(an[:, t, :], ps_a(t, g), ACT.Square, accum_out=mag2[:, t:t + 1])
                last.then_inc(mag2_done, 1)

            def n_hi_(k, s):
                done(act, nmp_mm, k)
                done(act, in_mm, k - 2)
                act.activation(n_hi[s][:, :], ps_nmp, ACT.Copy).then_inc(n_hi_done, 1)

            def imag_row_(k, g=None):
                done(act, imag_mm, k, g)
                act.activation(imag_row[:, cols(g)], ps_imag(g)[:, cols(g)], ACT.Copy).then_inc(imag_row_done, 1)

            def gates(k, g=None):
                c = cols(g)
                done(act, r_mm, k)
                done(act, r_g_done, k - 1)
                act.activation(r_t[:, c], ps_r[:, c], ACT.Tanh, scale=0.5, bias=gate_b[:, 0:1]).then_inc(r_t_done, 1)
                done(act, z_mm, k)
                done(act, z_g_done, k - 1)
                act.activation(z_t[:, c], ps_z[:, c], ACT.Tanh, scale=0.5, bias=gate_b[:, 1:2]).then_inc(z_t_done, 1)

            def prob_(k, g=None):
                done(act, nmax_done, k, g)
                done(act, probT_mm, k - 1)
                for t in each(g):
                    last = act.activation(prob[:, t, :], att[:, t, :], ACT.Exp, bias=nmax[:, t:t + 1],
                                          accum_out=rsum[:, t:t + 1])
                last.then_inc(prob_done, 1)

            def step(i, s):
                nxt = 1 - s
                nn_(i - 1)
                if has(i + 1):
                    h_rows(i + 1, nxt)
                common_(i)
                if has(i - 2):
                    probT_(i - 2)
                if has(i + 1):
                    c1_rows(i + 1, nxt)
                    dist_operands(i + 1)
                    msg_hi_(i + 1)
                h2T_(i - 1)
                if has(i + 1):
                    exp_dist(i + 1)
                xp_hi_(i - 1)
                if has(i + 1):
                    a0T_hi_(i + 1)
                if has(i - 2):
                    u_exp_(i - 2)
                    u_pos_(i - 2)
                row_norms(i - 1)
                if has(i + 1):
                    n_hi_(i + 1, nxt)
                    d_hi_(i + 1, nxt)
                imag_row_(i - 1)
                gates(i)
                prob_(i - 1)

            act.dma_start(vecs[:, :], vec).then_inc(w_vec, 16)
            act.dma_start(c2_w[:, :, :], w_c2).then_inc(w_conv2, 16)
            act.dma_start(se_b[:, :], b_se.broadcast_to([P, S])).then_inc(w_seb, 16)
            act.dma_start(msg_b[:, :], b_msg.broadcast_to([P, D])).then_inc(w_seb, 16)
            h_rows(0, 0)
            act.wait_ge(sums_made, 2)
            act.activation(c2_sh[:, :, :], c2_s[:, :, :], ACT.Copy).then_inc(conv2_hi, 1)
            act.wait_ge(consts_made, 1)
            c1_rows(0, 0)
            act.activation(c2_wh[:, :, :], c2_w[:, :, :], ACT.Copy).then_inc(conv2_hi, 1)
            act.dma_start(g_w[:, 0:2, :], w_ih).then_inc(w_gate, 16)
            act.dma_start(g_w[:, 2, :], w_hh).then_inc(w_gate, 16)
            act.dma_start(a_w[:, :], w_a).then_inc(w_back, 16)
            act.dma_start(att_b[:, :], bias.broadcast_to([P, D])).then_inc(w_back, 16)
            h_rows(1, 1)
            dist_operands(0)
            d_hi_(0, 0)
            msg_hi_(0)
            exp_dist(0)
            a0T_hi_(0)
            common_(0)
            c1_rows(1, 1)
            act.wait_ge(w_gate, 32)
            act.activation(g_wh[:, :, :], g_w[:, :, :], ACT.Copy).then_inc(gate_hi, 1)
            n_hi_(0, 0)
            dist_operands(1)
            msg_hi_(1)
            exp_dist(1)
            d_hi_(1, 1)
            a0T_hi_(1)
            n_hi_(1, 1)
            gates(0)
            steps(act, step)
            nn_(LAST - 1)
            common_(LAST)
            probT_(LAST - 2)
            h2T_(LAST - 1)
            u_exp_(LAST - 2)
            xp_hi_(LAST - 1)
            u_pos_(LAST - 2)
            row_norms(LAST - 1)
            imag_row_(LAST - 1)
            for g in range(G):
                gates(LAST, g)
            prob_(LAST - 1)
            nn_(LAST, 0)
            probT_(LAST - 1)
            nn_(LAST, 1)
            for g in range(G):
                h2T_(LAST, g)
            u_exp_(LAST - 1)
            for g in range(G):
                xp_hi_(LAST, g)
            u_pos_(LAST - 1)
            for g in range(G):
                row_norms(LAST, g)
            for g in range(G):
                imag_row_(LAST, g)
            for g in range(G):
                prob_(LAST, g)
            for g in range(G):
                probT_(LAST, g)
            for g in range(G):
                u_exp_(LAST, g)
                u_pos_(LAST, g)

        @block.vector
        def _(dve):
            def carry_wait(k):
                if not isinstance(k, int):
                    nc.vector.memset(tick_v[:, :], 0.0)

            def gru_w(k, g=None):
                c = cols(g)
                done(dve, r_g_done, k, g)
                done(dve, in_mm, k)
                nc.vector.scalar_tensor_tensor(gq[:, c], ps_hn[:, c], vecs[:, BH_N:BH_N + 1], r_g[:, c],
                                               ALU.add, ALU.mult).then_inc(gq_done, 1)
                done(dve, gq_done, k, g)
                nc.vector.tensor_tensor(gw[:, c], ps_in[:, c], gq[:, c], ALU.add).then_inc(gw_done, 1)

            def gru_(k, s, g=None):
                c = cols(g)
                done(dve, nn_done, k, g)
                nc.vector.tensor_tensor(dd[:, c], hT[s][:, c], nn[:, c], ALU.subtract).then_inc(dd_done, 1)
                done(dve, dd_done, k, g)
                done(dve, z_g_done, k, g)
                nc.vector.tensor_tensor(dd[:, c], z_g[:, c], dd[:, c], ALU.mult).then_inc(zd_done, 1)
                done(dve, zd_done, k, g)
                nc.vector.tensor_tensor(gru[:, c], nn[:, c], dd[:, c], ALU.add).then_inc(gru_done, 1)

            def stats1(k, s):
                moved(dve, x_loaded, k, s)
                for t in range(T):
                    last = nc.vector.bn_stats(stat1[:, t, :], x_in[s][:, t, :])
                last.then_inc(stat1_done, 1)

            def moments1(k):
                done(dve, stat1_done, k)
                carry_wait(k)
                for t in range(T):
                    last = nc.vector.bn_aggr(mv1[:, t, :], stat1[:, t, :])
                last.then_inc(mv1_done, 1)

            def xn1_(k, s):
                done(dve, rstd1_done, k)
                done(dve, hT_mm, k - 1)
                for t in range(T):
                    last = nc.vector.tensor_scalar(xn1[:, t, :], x_in[s][:, t, :], mv1[:, t, 0:1],
                                                   rstd1[:, t:t + 1], ALU.subtract, ALU.mult)
                last.then_inc(xn1_done, 1)

            def h_lo_(k, s):
                done(dve, h_hi_done, k)
                nc.vector.tensor_tensor(h_lo[s][:, :], hT[s][:, :], h_hi[s][:, :].bitcast(fp32),
                                        ALU.subtract).then_inc(h_lo_done, 1)

            def residual1(k, s, g=None):
                t = tl(g)
                done(dve, gruT_mm, k, g)
                moved(dve, res_loaded, k, s)
                nc.vector.tensor_tensor(x1[s][:, t, :], ps_gruT(g)[:, t, :], x_res[s][:, t, :],
                                        ALU.add).then_inc(x1_done, 1)
                done(dve, x1_done, k, g)
                for t in each(g):
                    last = nc.vector.bn_stats(stat2[:, t, :], x1[s][:, t, :])
                last.then_inc(stat2_done, 1)
                done(dve, stat2_done, k, g)
                carry_wait(k)
                for t in each(g):
                    last = nc.vector.bn_aggr(mv2[:, t, :], stat2[:, t, :])
                last.then_inc(mv2_done, 1)

            def embedding(k):
                done(dve, msg_mm, k)
                nc.vector.tensor_tensor(emb[:, :, :], ps_msg[:, :, D:D + S],
                                        se_b[:, :].unsqueeze(1).broadcast_to([P, T, S]),
                                        ALU.add).then_inc(emb_done, 1)
                done(dve, emb_done, k)
                done(dve, lrT_mm, k - 1)
                emb_2 = emb[:, :, :].unsqueeze(2).broadcast_to([P, T, 2, S])
                left = lr[:, :, 0, 0:4 * S].rearrange("p t (h c s) -> p t h c s", h=2, c=2)
                right = lr[:, :, 1, 0:4 * S].rearrange("p t (c h s) -> p t h c s", h=2, c=2)
                nc.vector.tensor_copy(left[:, :, 0].bitcast(f32r), emb_2)
                nc.vector.tensor_copy(right[:, :, 0].bitcast(f32r), emb_2)
                nc.vector.tensor_tensor(emb_sq[:, :, :], emb[:, :, :], emb[:, :, :],
                                        ALU.mult).then_inc(emb_hi_done, 1)
                done(dve, emb_hi_done, k)
                nc.vector.tensor_tensor(left[:, :, 1], emb_2, left[:, :, 0], ALU.subtract)
                nc.vector.tensor_tensor(right[:, :, 1], emb_2, right[:, :, 0], ALU.subtract)
                nc.vector.reduce_sum(emb_q[:, :, :], emb_sq[:, :, :],
                                     mybir.AxisListType.X).then_inc(emb_q_done, 1)
                done(dve, emb_q_done, k)
                sides = lr[:, :, :, :].rearrange("p t a q -> p t (a q)")
                q_hi = sides[:, :, LR - 4:LR - 1 + Q:Q + 2]
                q_lo = sides[:, :, LR - 3:LR + Q:Q + 2]
                q_2 = emb_q[:, :, :].broadcast_to([P, T, 2])
                nc.vector.tensor_copy(q_hi.bitcast(f32r), q_2).then_inc(q_hi_done, 1)
                done(dve, q_hi_done, k)
                nc.vector.tensor_tensor(q_lo, q_2, q_hi, ALU.subtract).then_inc(lr_done, 1)

            def messages(k):
                done(dve, emb_q_done, k)
                nc.vector.tensor_tensor(msg0[:, :, :], ps_msg[:, :, 0:D],
                                        msg_b[:, :].unsqueeze(1).broadcast_to([P, T, D]),
                                        ALU.add).then_inc(msg0_done, 1)

            def msg_lo_(k):
                done(dve, msg_hi_done, k)
                nc.vector.scalar_tensor_tensor(msg_lo[:, :, :], msg0[:, :, :], 0.0, msg_hi[:, :, :].bitcast(fp32),
                                               ALU.max, ALU.subtract).then_inc(msg_lo_done, 1)

            def h2_(k, s, g=None):
                done(dve, rstd2_done, k, g)
                for t in each(g):
                    last = nc.vector.tensor_scalar(h2[s][:, t, :], x1[s][:, t, :], mv2[:, t, 0:1],
                                                   rstd2[:, t:t + 1], ALU.subtract, ALU.mult)
                last.then_inc(h2n_done, 1)
                done(dve, h2n_done, k, g)
                nc.vector.tensor_scalar(h2[s][:, tl(g), :], h2[s][:, tl(g), :], 0.0, None,
                                        ALU.max).then_inc(h2_done, 1)

            def attended(k, g=None):
                done(dve, prob_done, k, g)
                nc.vector.reciprocal(rinv[:, tl(g)], rsum[:, tl(g)]).then_inc(rinv_done, 1)
                done(dve, rinv_done, k, g)
                done(dve, pv_mm, k, g)
                for t in each(g):
                    last = nc.vector.scalar_tensor_tensor(u_att[:, t, :], ps_pv(g)[:, t, :], rinv[:, t:t + 1],
                                                          att_b[:, :], ALU.mult, ALU.add)
                last.then_inc(u_done, 1)

            def a0T_(k):
                done(dve, ed_done, k)
                done(dve, adjT_mm, k)
                done(dve, a0T_lo_done, k - 1)
                nc.vector.tensor_tensor(a0T[:, :, :], ps_adjT, ed[:, :, :], ALU.mult).then_inc(a0T_done, 1)

            def xp_lo_(k, g=None):
                done(dve, xp_hi_done, k, g)
                for h in range(G) if g is None else (g,):
                    nc.vector.tensor_tensor(xp_lo[:, cols(h)], ps_xp(g)[:, cols(h)], xp_hi[:, cols(h)].bitcast(fp32),
                                            ALU.subtract).then_inc(xp_lo_done, 1)

            def residual2(k, s, g=None):
                t = tl(g)
                done(dve, u_pos_done, k, g)
                nc.vector.scalar_tensor_tensor(u_pos[:, t, :], u_exp[:, t, :], 1.0, u_pos[:, t, :],
                                               ALU.min, ALU.add).then_inc(u_elu_done, 1)
                done(dve, u_elu_done, k, g)
                moved(dve, stored, k, s)
                nc.vector.scalar_tensor_tensor(y_out[s][:, t, :], u_pos[:, t, :], -1.0,
                                               x1[s][:, t, :], ALU.add, ALU.add).then_inc(y_done, 1)

            def neg_(k, s):
                moved(dve, adj_loaded, k, s)
                nc.vector.tensor_scalar(neg[s][:, :, :], adj_in[s][:, :, :], 0.0, MASKED,
                                        ALU.is_le, ALU.mult).then_inc(neg_done, 1)

            def n_lo_(k, s):
                done(dve, n_hi_done, k)
                nc.vector.tensor_tensor(n_lo[s][:, :], ps_nmp, n_hi[s][:, :].bitcast(fp32),
                                        ALU.subtract).then_inc(n_lo_done, 1)

            def by_parity(rows):
                return rows.rearrange("p (g j q) -> p g j q", g=G, q=2)

            def conv2_rows(k, s):
                done(dve, conv2_mm, k)
                done(dve, hb_done, k)
                nc.vector.scalar_tensor_tensor(
                    by_parity(c2[:, :]), ps_conv2.rearrange("p (q g j) -> p g j q", q=2, g=G), bn_s[:, 1:2],
                    by_parity(hb[:, :]), ALU.mult, ALU.add).then_inc(c2_done, 1)
                done(dve, c2_done, k)
                nc.vector.tensor_scalar(c_hi[:, :], c2[:, :], 0.0, None, ALU.max).then_inc(c_hi_done, 1)
                done(dve, c_hi_done, k)
                nc.vector.scalar_tensor_tensor(c_lo[:, :], c2[:, :], 0.0, c_hi[:, :].bitcast(fp32),
                                               ALU.max, ALU.subtract).then_inc(c_lo_done, 1)

            def scores(k, s, g=None):
                ts = tl(g)
                done(dve, imag_row_done, k, g)
                for t in each(g):
                    last = nc.vector.scalar_tensor_tensor(
                        an[:, t, :], ps_a(t, g), imag[:, t:t + 1],
                        imag_row[:, (t // NT) * N:(t // NT + 1) * N], ALU.mult, ALU.mult)
                last.then_inc(an_done, 1)
                done(dve, an_done, k, g)
                nc.vector.scalar_tensor_tensor(score[:, ts, :], an[:, ts, :], SLOPE, an[:, ts, :],
                                               ALU.mult, ALU.max).then_inc(score_done, 1)
                done(dve, score_done, k, g)
                done(dve, neg_done, k)
                carry_wait(k)
                for t in each(g):
                    last = nc.vector.tensor_tensor_reduce(
                        out=att[:, t, :], in0=score[:, t, :], in1=neg[s][:, t, :], scale=1.0,
                        scalar=MASKED, op0=ALU.add, op1=ALU.max, accum_out=rmax[:, t:t + 1])
                last.then_inc(att_done, 1)
                done(dve, att_done, k, g)
                nc.vector.tensor_scalar(nmax[:, ts], rmax[:, ts], -1.0, None, ALU.mult).then_inc(nmax_done, 1)

            def step(i, s):
                nxt = 1 - s
                gru_w(i - 1)
                if has(i + 2):
                    stats1(i + 2, s)
                gru_(i - 1, nxt)
                if has(i + 1):
                    h_lo_(i + 1, nxt)
                if has(i + 2):
                    moments1(i + 2)
                residual1(i - 1, nxt)
                if has(i + 1):
                    embedding(i + 1)
                    messages(i + 1)
                h2_(i - 1, nxt)
                if has(i - 2):
                    attended(i - 2)
                if has(i + 1):
                    msg_lo_(i + 1)
                    a0T_(i + 1)
                xp_lo_(i - 1)
                neg_(i, s)
                if has(i - 2):
                    residual2(i - 2, s)
                if has(i + 2):
                    xn1_(i + 2, s)
                conv2_rows(i, s)
                if has(i + 1):
                    n_lo_(i + 1, nxt)
                scores(i - 1, nxt)

            nc.vector.memset(dl[:, :].bitcast(fp32), 0.0)
            nc.vector.memset(dr[:, :].bitcast(fp32), 0.0)
            nc.vector.memset(lr[:, :, :, :], 0.0).then_inc(dist_consts, 1)
            dve.wait_ge(dist_consts, 1)
            nc.vector.memset(lr[:, :, 1, LR - 4:LR - 2], -0.5)
            nc.vector.memset(lr[:, :, 0, LR - 2:LR], -0.5).then_inc(dist_consts, 1)
            stats1(0, 0)
            moments1(0)
            xn1_(0, 0)
            dve.wait_ge(w_conv1, 16)
            nc.vector.tensor_copy(c1_wh[:, :], c1_w[:, :]).then_inc(conv1_hi, 1)
            dve.wait_ge(conv1_hi, 1)
            nc.vector.tensor_tensor(c1_wl[:, :], c1_w[:, :], c1_wh[:, :].bitcast(fp32),
                                    ALU.subtract).then_inc(conv1_lo, 1)
            stats1(1, 1)
            moments1(1)
            dve.wait_ge(w_conv2, 16)
            nc.vector.tensor_copy(c2_s[:, 0, :], c2_w[:, 0, :]).then_inc(sums_made, 1)
            nc.vector.tensor_tensor(c2_s[:, 1:EVEN, :], c2_w[:, 2:TAPS:2, :], c2_w[:, 1:TAPS:2, :],
                                    ALU.add).then_inc(sums_made, 1)
            h_lo_(0, 0)
            xn1_(1, 1)
            dve.wait_ge(conv2_hi, 1)
            nc.vector.tensor_tensor(c2_sl[:, :, :], c2_s[:, :, :], c2_sh[:, :, :].bitcast(fp32),
                                    ALU.subtract).then_inc(conv2_lo, 1)
            dve.wait_ge(w_seb, 32)
            dve.wait_ge(dist_consts, 2)
            embedding(0)
            messages(0)
            dve.wait_ge(conv2_hi, 2)
            nc.vector.tensor_tensor(c2_wl[:, :, :], c2_w[:, :, :], c2_wh[:, :, :].bitcast(fp32),
                                    ALU.subtract).then_inc(conv2_lo, 1)
            msg_lo_(0)
            h_lo_(1, 1)
            a0T_(0)
            n_lo_(0, 0)
            embedding(1)
            messages(1)
            stats1(2, 0)
            moments1(2)
            msg_lo_(1)
            a0T_(1)
            xn1_(2, 0)
            neg_(0, 0)
            conv2_rows(0, 0)
            n_lo_(1, 1)
            dve.wait_ge(w_back, 32)
            steps(dve, step)
            gru_w(LAST - 1)
            gru_(LAST - 1, 0)
            residual1(LAST - 1, 0)
            h2_(LAST - 1, 0)
            attended(LAST - 2)
            xp_lo_(LAST - 1)
            residual2(LAST - 2, 1)
            neg_(LAST, 1)
            conv2_rows(LAST, 1)
            scores(LAST - 1, 0)
            for g in range(G):
                gru_w(LAST, g)
            for g in range(G):
                gru_(LAST, 1, g)
            for g in range(G):
                residual1(LAST, 1, g)
            for g in range(G):
                h2_(LAST, 1, g)
            attended(LAST - 1)
            for g in range(G):
                xp_lo_(LAST, g)
            residual2(LAST - 1, 0)
            for g in range(G):
                scores(LAST, 1, g)
            for g in range(G):
                attended(LAST, g)
            for g in range(G):
                residual2(LAST, 1, g)

        @block.tensor
        def _(pe):
            def product(out, w_hi, w_lo, v_hi, v_lo, start=True, stop=True):
                nc.tensor.matmul(out, w_hi, v_hi, start=start, stop=False)
                nc.tensor.matmul(out, w_hi, v_lo, start=False, stop=False)
                return nc.tensor.matmul(out, w_lo, v_hi, start=False, stop=stop)

            def hT_(k):
                done(pe, xn1_done, k)
                done(pe, an_done, k - 3)
                done(pe, h_hi_done, k - 1)
                for t in range(T):
                    last = nc.tensor.transpose(ps_hT[:, t * P:(t + 1) * P], xn1[:, t, :], ident[:, :])
                last.then_inc(hT_mm, 1)

            def conv1(k, s):
                done(pe, h_lo_done, k)
                done(pe, gw_done, k - 2)
                done(pe, ed_done, k - 1)
                product(ps_conv1, c1_wh[:, :], c1_wl[:, :], h_hi[s][:, :], h_lo[s][:, :]).then_inc(conv1_mm, 1)

            def messages(k, s):
                done(pe, hT_done, k)
                done(pe, gw_done, k - 2)
                done(pe, ed_done, k - 1)
                done(pe, n_lo_done, k - 1)
                done(pe, common_done, k - 1)
                for t in range(T):
                    last = nc.tensor.matmul(ps_msg[:, t, :], hT[s][:, t * P:(t + 1) * P],
                                            msg_w[:, :], start=True, stop=True)
                last.then_inc(msg_mm, 1)

            def lrT_(k):
                done(pe, lr_done, k)
                done(pe, x1_done, k - 2)
                done(pe, an_done, k - 3)
                for t in range(T):
                    last = nc.tensor.transpose(ps_lrT[:, t * P:(t + 1) * P],
                                               lr[:, t, :, :].rearrange("p a q -> p (a q)"), ident[:, :])
                last.then_inc(lrT_mm, 1)

            def dist(k):
                done(pe, lrT_done, k)
                done(pe, c1_hi_done, k)
                done(pe, msg0_done, k)
                for t in range(T):
                    last = nc.tensor.matmul(ps_dist[:, t, :], dl[:, t * P:(t + 1) * P], dr[:, cols(t // NT)],
                                            start=True, stop=True)
                last.then_inc(dist_mm, 1)

            def adjT(k, s):
                moved(pe, adj_loaded, k, s)
                done(pe, probT_done, k - 3)
                done(pe, r_t_done, k - 2)
                done(pe, z_t_done, k - 2)
                done(pe, a0T_done, k - 1)
                for t in range(T):
                    for m in range(NT):
                        last = nc.tensor.transpose(
                            ps_adjT[:, t // NT * NT + m, (t % NT) * P:(t % NT + 1) * P],
                            adj_in[s][:, t, m * P:(m + 1) * P], ident[:, :])
                last.then_inc(adjT_mm, 1)

            def nmp(k):
                done(pe, a0T_lo_done, k)
                done(pe, msg_lo_done, k)
                done(pe, h2T_done, k - 2)
                done(pe, msg0_done, k)
                for g in range(G):
                    for m in range(NT):
                        t = g * NT + m
                        last = product(ps_nmp[:, cols(g)], msg_hi[:, t, :], msg_lo[:, t, :],
                                       a0T_hi[:, t, :], a0T_lo[:, t, :], start=(m == 0), stop=(m == NT - 1))
                last.then_inc(nmp_mm, 1)

            def conv2(k, s, first, end):
                for n in range(first, end):
                    if n < EVEN:
                        if n == 0:
                            done(pe, c1_lo_done, k)
                            done(pe, msg0_done, k)
                            if not isinstance(k, int) or k > 0:
                                done(pe, n_lo_done, k)
                        m, source, out = n, 0, ps_common
                        w_hi, w_lo, shift, end_of = c2_sh[:, m, :], c2_sl[:, m, :], m, EVEN
                    elif n < EVEN + ODD:
                        if n == EVEN:
                            done(pe, d_lo_done, k)
                            done(pe, c2_done, k - 1)
                        m, source, out = n - EVEN, 1, ps_conv2[:, 0:N]
                        w_hi, w_lo, shift, end_of = c2_wh[:, 2 * m + 1, :], c2_wl[:, 2 * m + 1, :], m + 1, ODD
                    else:
                        m, source, out = n - EVEN - ODD, 2, ps_conv2[:, N:2 * N]
                        w_hi, w_lo, shift, end_of = c2_wh[:, 2 * m, :], c2_wl[:, 2 * m, :], m, EVEN
                    of = slice(shift, shift + H)
                    last = product(out, w_hi, w_lo, cv_hi[s][:, source, :, of], cv_lo[s][:, source, :, of],
                                   start=(m == 0), stop=(m == end_of - 1))
                    if n == EVEN - 1:
                        last.then_inc(common_mm, 1)
                if end == PASSES:
                    last.then_inc(conv2_mm, 1)

            def gate(out, source, part, v_hi, v_lo, start, stop):
                c = slice(part * D, (part + 1) * D)
                return product(out, g_wh[:, source, c], g_wl[:, source, c], v_hi, v_lo, start, stop)

            def gates_n(k, s):
                h = h_hi[s][:, :], h_lo[s][:, :]
                ne = n_hi[s][:, :], n_lo[s][:, :]
                done(pe, n_lo_done, k)
                done(pe, gw_done, k - 1)
                done(pe, ed_done, k + 1)
                gate(ps_hn, 2, 2, *h, True, True)
                gate(ps_in, 1, 2, *ne, True, False)

            def gate_r(k, s):
                h = h_hi[s][:, :], h_lo[s][:, :]
                ne = n_hi[s][:, :], n_lo[s][:, :]
                done(pe, probT_done, k - 2)
                done(pe, r_t_done, k - 1)
                done(pe, a0T_done, k + 1)
                gate(ps_r, 2, 0, *h, True, False)
                gate(ps_r, 1, 0, *ne, False, False)

            def gate_z(k, s):
                h = h_hi[s][:, :], h_lo[s][:, :]
                ne = n_hi[s][:, :], n_lo[s][:, :]
                done(pe, imag_row_done, k - 1)
                done(pe, z_t_done, k - 1)
                gate(ps_z, 2, 1, *h, True, False)
                gate(ps_z, 1, 1, *ne, False, False)

            def gates_c(k):
                co = c_hi[:, :], c_lo[:, :]
                done(pe, c_lo_done, k)
                gate(ps_r, 0, 0, *co, False, True).then_inc(r_mm, 1)
                gate(ps_z, 0, 1, *co, False, True).then_inc(z_mm, 1)
                gate(ps_in, 0, 2, *co, False, True).then_inc(in_mm, 1)

            def probT_(k, g=None, gates_read=None):
                done(pe, prob_done, k, g)
                if g is None:
                    done(pe, r_t_done, k + 1, gates_read)
                    done(pe, z_t_done, k + 1, gates_read)
                else:
                    done(pe, probT_done, k - 1)
                for t in each(g):
                    for m in range(NT):
                        last = nc.tensor.transpose(
                            ps_probT[:, t // NT * NT + m, (t % NT) * P:(t % NT + 1) * P],
                            prob[:, t, m * P:(m + 1) * P], ident[:, :])
                last.then_inc(probT_mm, 1)

            def gruT_(k, g=None):
                done(pe, gru_done, k, g)
                done(pe, an_done, k - 1)
                for t in each(g):
                    last = nc.tensor.transpose(ps_gruT(g)[:, t, :], gru[:, t * P:(t + 1) * P], ident[:, :])
                last.then_inc(gruT_mm, 1)

            def pv(k, s, g=None):
                done(pe, probT_done, k, g)
                if g is None:
                    done(pe, h_hi_done, k + 3)
                    done(pe, an_done, k)
                else:
                    half_done(pe, xp_lo_done, k, g)
                for t in each(g):
                    for m in range(NT):
                        r = t // NT * NT + m
                        last = nc.tensor.matmul(ps_pv(g)[:, t, :], probT[:, r, (t % NT) * P:(t % NT + 1) * P],
                                                h2[s][:, r, :], start=(m == 0), stop=(m == NT - 1))
                last.then_inc(pv_mm, 1)

            def h2T_(k, s, g=None):
                done(pe, h2_done, k, g)
                if g is None:
                    done(pe, msg0_done, k + 2)
                    done(pe, common_done, k + 1)
                else:
                    done(pe, c2_done, k)
                    done(pe, x1_done, k, 0)
                for t in each(g):
                    last = nc.tensor.transpose(ps_h2T(g)[:, t * P:(t + 1) * P], h2[s][:, t, :], ident[:, :])
                last.then_inc(h2T_mm, 1)

            def xp(k, g=None):
                done(pe, h2T_done, k, g)
                if g is None:
                    done(pe, u_done, k - 1)
                    done(pe, h_hi_done, k + 2)
                else:
                    done(pe, gw_done, k, G - 1)
                nc.tensor.matmul(ps_xp(g)[:, cols(g)], a_w[:, :], h2T[:, cols(g)],
                                 start=True, stop=True).then_inc(xp_mm, 1)

            def scores(k, g=None):
                if g is None:
                    done(pe, x1_done, k)
                    done(pe, lrT_done, k + 2)
                    half_done(pe, xp_lo_done, k, G - 1)
                else:
                    done(pe, h2T_done, k, g)
                for h in range(G) if g is None else (g,):
                    half_done(pe, xp_lo_done, k, h)
                    for t in each(h):
                        last = product(ps_a(t, g), xp_hi[:, t * P:(t + 1) * P], xp_lo[:, t * P:(t + 1) * P],
                                       xp_hi[:, cols(h)], xp_lo[:, cols(h)])
                    last.then_inc(a_mm, 1)

            def imag_row_(k, g=None):
                done(pe, imag_done, k, g)
                if g is None:
                    done(pe, a0T_done, k + 2)
                    done(pe, probT_done, k - 1)
                else:
                    done(pe, x1_done, k, G - 1)
                    done(pe, u_done, k - 1)
                for t in each(g):
                    last = nc.tensor.transpose(ps_imag(g)[:, t * P:(t + 1) * P],
                                               imag[:, t:t + 1].broadcast_to([P, P]), ident[:, :])
                last.then_inc(imag_mm, 1)

            def step(i, s):
                nxt = 1 - s
                conv2(i, s, 0, 9)
                if has(i + 1):
                    hT_(i + 1)
                conv2(i, s, 9, 12)
                if has(i - 2):
                    probT_(i - 2)
                conv2(i, s, 12, 16)
                gruT_(i - 1)
                if has(i + 1):
                    conv1(i + 1, nxt)
                    messages(i + 1, nxt)
                if has(i - 2):
                    pv(i - 2, s)
                conv2(i, s, 16, 17)
                if has(i + 1):
                    lrT_(i + 1)
                    adjT(i + 1, nxt)
                conv2(i, s, 17, 18)
                h2T_(i - 1, nxt)
                if has(i + 1):
                    dist(i + 1)
                conv2(i, s, 18, 20)
                xp(i - 1)
                conv2(i, s, 20, 21)
                gates_n(i, s)
                conv2(i, s, 21, 22)
                scores(i - 1)
                conv2(i, s, 22, PASSES)
                if has(i + 1):
                    nmp(i + 1)
                imag_row_(i - 1)
                gate_r(i, s)
                gate_z(i, s)
                gates_c(i)

            pe.wait_ge(ident_made, 1)
            hT_(0)
            pe.wait_ge(conv1_lo, 1)
            conv1(0, 0)
            pe.wait_ge(w_message, 16)
            messages(0, 0)
            hT_(1)
            lrT_(0)
            adjT(0, 0)
            pe.wait_ge(pads_made, 1)
            pe.wait_ge(conv2_lo, 1)
            conv2(0, 0, 0, 3)
            dist(0)
            conv2(0, 0, 3, 6)
            conv1(1, 1)
            conv2(0, 0, 6, EVEN)
            pe.wait_ge(conv2_lo, 2)
            conv2(0, 0, EVEN, 14)
            done(pe, common_done, 0)
            nmp(0)
            conv2(0, 0, 14, 18)
            messages(1, 1)
            conv2(0, 0, 18, 21)
            lrT_(1)
            adjT(1, 1)
            conv2(0, 0, 21, 23)
            dist(1)
            conv2(0, 0, 23, PASSES)
            pe.wait_ge(gate_lo, 1)
            gates_n(0, 0)
            gate_r(0, 0)
            gate_z(0, 0)
            nmp(1)
            gates_c(0)
            pe.wait_ge(w_back, 32)
            steps(pe, step)
            conv2(LAST, 1, 0, 6)
            probT_(LAST - 2)
            conv2(LAST, 1, 6, 11)
            gruT_(LAST - 1)
            pv(LAST - 2, 1)
            conv2(LAST, 1, 11, 21)
            h2T_(LAST - 1, 0)
            conv2(LAST, 1, 21, 23)
            xp(LAST - 1)
            conv2(LAST, 1, 23, PASSES)
            scores(LAST - 1)
            gates_n(LAST, 1)
            gate_r(LAST, 1)
            imag_row_(LAST - 1)
            gate_z(LAST, 1)
            gates_c(LAST)
            probT_(LAST - 1, gates_read=G - 1)
            for g in range(G):
                gruT_(LAST, g)
            pv(LAST - 1, 0)
            for g in range(G):
                h2T_(LAST, 1, g)
            for g in range(G):
                xp(LAST, g)
            for g in range(G):
                scores(LAST, g)
            for g in range(G):
                imag_row_(LAST, g)
            for g in range(G):
                probT_(LAST, g)
            for g in range(G):
                pv(LAST, 1, g)


def kernel(**inputs):
    import numpy as np
    import concourse.bacc as bacc
    from concourse.bass_utils import run_bass_kernel_spmd

    def a(name):
        return np.asarray(inputs[name])

    def g(name):
        return a("L0_gnn_" + name)

    rows = [g(f"bn{n}_{v}") for n in (1, 2) for v in "gbmv"]
    rows += list(g("b_ih").reshape(3, D)) + list(g("b_hh").reshape(3, D))
    arrays = {
        "x": a("x"),
        "adj": a("adj"),
        "vec": np.stack(rows, axis=1),
        "b_se": g("b_se").reshape(1, S),
        "w_c1": g("conv1_w")[:, :, 0].T,
        "w_c2": g("conv2_w").transpose(1, 2, 0),
        "w_msg": np.concatenate([g("w_msg").T, g("w_se").T], axis=1),
        "b_msg": g("b_msg").reshape(1, D),
        "w_ih": g("w_ih").reshape(3 * D, 2, D).transpose(2, 1, 0),
        "w_hh": g("w_hh").T,
        "w_a": a("L1_gnn_W_a"),
        "bias": a("L1_gnn_bias").reshape(1, D),
    }
    arrays = {f"{n}_dram": np.ascontiguousarray(v) for n, v in arrays.items()}
    nc = bacc.Bacc("TRN2", target_bir_lowering=False, num_devices=1)
    args = [nc.dram_tensor(n, v.shape, mybir.dt.from_np(v.dtype), kind="ExternalInput").ap()
            for n, v in arrays.items()]
    out = nc.dram_tensor("out_dram", (B, N, D), mybir.dt.float32, kind="ExternalOutput").ap()
    build(nc, *args, out)
    r = run_bass_kernel_spmd(nc, [arrays], core_ids=[0])
    return r.results[0]["out_dram"]
```
